# Optimizing a Trainium2 kernel written in Bass

```python
import numpy as np
import jax
import jax.numpy as jnp

def _softmax(x, axis=-1):
    return jax.nn.softmax(x, axis=axis)

def _gelu(x):
    return jax.nn.gelu(x, approximate=True)

def _silu(x):
    return jax.nn.silu(x)

def _sigmoid(x):
    return jax.nn.sigmoid(x)

def _layernorm(x, axis=-1, eps=1e-05):
    m = jnp.mean(x, axis=axis, keepdims=True)
    v = jnp.var(x, axis=axis, keepdims=True)
    return (x - m) / jnp.sqrt(v + eps)

def _scatter_add(tgt, idx, src, axis=0):
    return tgt.at[idx].add(src)

def _segment_sum(src, seg, n):
    return jax.ops.segment_sum(src, seg, n)
kernel_name = 'mk_flamingo_gated_d1_seqx_r8_04e664'

def setup_inputs(seed: int=0):
    np.random.seed(seed)
    _w = jnp.asarray

    def _rec_inputs():
        import jax
        import jax.numpy as jnp
        _rk = jax.random.key(seed)
        x = -0.0003929 + 0.9999 * jax.random.normal(jax.random.fold_in(_rk, 1), (32, 64, 512), jnp.float32)
        _lenS = 64 - jax.random.randint(jax.random.fold_in(_rk, 7), (32,), 0, max(1, 64 // 4) + 1, jnp.int32)
        _lenS2 = 64 - jax.random.randint(jax.random.fold_in(_rk, 8), (32,), 0, max(1, 64 // 4) + 1, jnp.int32)
        _ctx_1024P = jax.random.normal(jax.random.fold_in(_rk, 11), (32, 16, 128), jnp.float32)
        _ctx_1024c = jax.random.dirichlet(jax.random.fold_in(_rk, 511), 0.3 * jnp.ones((16,), jnp.float32), (32, 64))
        _ctx_1024t = jnp.einsum('bsk,bkd->bsd', _ctx_1024c, _ctx_1024P)
        _ctx_1024t = _ctx_1024t * jax.lax.rsqrt(jnp.mean(jnp.square(_ctx_1024t)) + 1e-12) * 0.953939
        ctx_1024 = -1.39393e-06 + 0.999914 * (_ctx_1024t + 0.3 * jax.random.normal(jax.random.fold_in(_rk, 611), (32, 64, 128), jnp.float32))
        _g = jax.random.normal(jax.random.fold_in(_rk, 9001), (2, 1), jnp.float32)
        _g = jnp.sign(_g) * jnp.maximum(jnp.abs(_g), 1.0) + (_g == 0) * 1.0
        g_xattn = _g[0]
        g_ffn = _g[1]
        return (x, ctx_1024, g_xattn, g_ffn)
    x, ctx_1024, g_xattn, g_ffn = _rec_inputs()

    def _L0_xattn_setup():
        import jax, jax.numpy as jnp
        import numpy as np
        import math
        DIM_V = 64
        key = jax.random.key(seed)
        k1, k2, k3, k4, k5, k6 = jax.random.split(key, 6)
        B, C, N, M = (8, DIM_V, 512, 128)
        pcd_up = jax.random.normal(k1, (B, C, N), dtype=jnp.float32)
        pcd_down = jax.random.normal(k2, (B, C, M), dtype=jnp.float32)
        s = 1.0 / math.sqrt(C)
        Wq = jax.random.normal(k3, (C, C), dtype=jnp.float32) * s
        Wk = jax.random.normal(k4, (C, C), dtype=jnp.float32) * s
        Wv = jax.random.normal(k5, (C, C), dtype=jnp.float32) * s
        Wskip = jax.random.normal(k6, (C, C), dtype=jnp.float32) * s
        return {'pcd_up': pcd_up, 'pcd_down': pcd_down, 'Wq': Wq, 'Wk': Wk, 'Wv': Wv, 'Wskip': Wskip}
    _L0_xattn_all = _L0_xattn_setup()
    _L0_xattn_in = {k: v for k, v in _L0_xattn_all.items() if k in ('Wq', 'Wk', 'Wv', 'Wskip')}
    del _L0_xattn_all

    def _L0_ffn_setup():
        import jax, jax.numpy as jnp
        import numpy as np
        BATCH, SEQ, D = (2, 256, 512)
        K, TOPK, RANK = (64, 16, 16)
        ALPHA = 32.0
        SCALING = ALPHA / RANK
        key = jax.random.key(seed)
        k1, k2, k3, k4 = jax.random.split(key, 4)
        x = jax.random.normal(k1, (BATCH, SEQ, D), dtype=jnp.float32)
        A = jax.random.normal(k2, (K, RANK, D), dtype=jnp.float32) * 0.02
        B = jax.random.normal(k3, (K, D, RANK), dtype=jnp.float32) * 0.02
        Wr = jax.random.normal(k4, (K, D), dtype=jnp.float32) * 0.02
        return {'x': x, 'A': A, 'B': B, 'Wr': Wr}
    _L0_ffn_all = _L0_ffn_setup()
    _L0_ffn_in = {k: v for k, v in _L0_ffn_all.items() if k in ('A', 'B', 'Wr')}
    del _L0_ffn_all
    return {'x': x, 'ctx_1024': ctx_1024, 'g_xattn': g_xattn, 'g_ffn': g_ffn, 'L0_xattn_Wq': _L0_xattn_in['Wq'], 'L0_xattn_Wk': _L0_xattn_in['Wk'], 'L0_xattn_Wv': _L0_xattn_in['Wv'], 'L0_xattn_Wskip': _L0_xattn_in['Wskip'], 'L0_ffn_A': _L0_ffn_in['A'], 'L0_ffn_B': _L0_ffn_in['B'], 'L0_ffn_Wr': _L0_ffn_in['Wr']}

def reference(x, ctx_1024, g_xattn, g_ffn, L0_xattn_Wq, L0_xattn_Wk, L0_xattn_Wv, L0_xattn_Wskip, L0_ffn_A, L0_ffn_B, L0_ffn_Wr):
    import jax
    import jax.numpy as jnp

    def _L0_xattn_ref(pcd_up, pcd_down, Wq, Wk, Wv, Wskip):
        import jax, jax.numpy as jnp
        import numpy as np
        import math
        DIM_V = 64
        q = jnp.einsum('oc,bcn->bon', Wq, pcd_up)
        k = jnp.einsum('oc,bcm->bom', Wk, pcd_down)
        v = jnp.einsum('oc,bcm->bom', Wv, pcd_down)
        C = q.shape[1]
        scale = jnp.sqrt(jnp.asarray(C, dtype=q.dtype))
        energy = jnp.einsum('bcn,bcm->bnm', q, k) / scale
        attention = jax.nn.softmax(energy, axis=-1)
        x = jnp.einsum('bnm,bcm->bcn', attention, v)
        skip = jnp.einsum('oc,bcn->bon', Wskip, pcd_up)
        return skip + x

    def _L0_ffn_ref(x, A, B, Wr):
        import jax, jax.numpy as jnp
        import numpy as np
        BATCH, SEQ, D = (2, 256, 512)
        K, TOPK, RANK = (64, 16, 16)
        ALPHA = 32.0
        SCALING = ALPHA / RANK
        prefix = x.shape[:-1]
        xf = x.reshape(-1, x.shape[-1])
        N = xf.shape[0]
        scores = xf @ Wr.T
        top_vals, top_idx = jax.lax.top_k(scores, TOPK)
        gates = jax.nn.softmax(top_vals, axis=-1)
        G = jnp.zeros((N, K), xf.dtype).at[jnp.arange(N)[:, None], top_idx].set(gates)
        h = jnp.einsum('nd,krd->nkr', xf, A)
        out = jnp.einsum('nkr,kdr->nd', h * G[:, :, None], B)
        return (out * SCALING).reshape(*prefix, -1)
    x = x + jnp.tanh(g_xattn[0]) * _L0_xattn_ref(_layernorm(x, axis=-1), ctx_1024, L0_xattn_Wq, L0_xattn_Wk, L0_xattn_Wv, L0_xattn_Wskip)
    x = x + jnp.tanh(g_ffn[0]) * _L0_ffn_ref(_layernorm(x, axis=-1), L0_ffn_A, L0_ffn_B, L0_ffn_Wr)
    return x

_drawn_inputs = setup_inputs


def setup_inputs(seed=0):
    import zlib

    import numpy as np

    out = dict(_drawn_inputs(seed))
    spreads = {}
    factors = {'L0_ffn_A': 3.868, 'L0_ffn_B': 3.667, 'L0_ffn_Wr': 4.202}
    for name, (base, spread) in spreads.items():
        noise = np.random.default_rng([zlib.crc32(name.encode()), seed]).standard_normal(out[name].shape)
        drawn = base * np.exp(spread * noise) if base else spread * noise
        out[name] = jnp.asarray(drawn.astype(out[name].dtype))
    for name, factor in factors.items():
        out[name] = (out[name] * factor).astype(out[name].dtype)
    return out
```

```python
from contextlib import ExitStack

import concourse.bass as bass
from concourse import mybir

F32 = mybir.dt.float32
F32R = mybir.dt.float32r
ALU = mybir.AluOpType
ACT = mybir.ActivationFunctionType
AX_X = mybir.AxisListType.X

P = 128
EPS = 1e-5
REPLACED = -3.0e38
FFN_SCALING = 32.0 / 16


class Tile:

    def __init__(self, number, rounds=None):
        self.number, self.rounds = number, rounds

    def __add__(self, k):
        return Tile(self.number + k, self.rounds)

    @property
    def parity(self):
        return self.number % 2

    def count(self, per_tile, more=0):
        fixed = per_tile * self.number + more
        return fixed if self.rounds is None else self.rounds * (2 * per_tile) + fixed

    def dma_count(self, more=0):
        fixed = 16 * (self.number // 2 + more)
        return fixed if self.rounds is None else self.rounds * 16 + fixed


def after(engine, semaphore, value):
    if not isinstance(value, int) or value > 0:
        engine.wait_ge(semaphore, value)


def after_apart(engine, semaphore, value):
    after(engine, semaphore, value)
    engine.nop(nofuse=True)


def flamingo_block(nc, x, ctx, g_xattn, g_ffn, Wq, Wk, Wv, Wskip, A, B, Wr, out):
    batches, C, N = x.shape
    M = ctx.shape[2]
    K, RANK, D = A.shape
    TILES = batches * C // P
    NCH = N // P
    DCH = D // P
    KR = K * RANK
    KCH = KR // P
    RPC = P // K
    TOP = 8
    H_BLOCKS = [(0, 6), (6, 12), (12, 17)]
    FIRST_FULL, LAST_FULL = 4, TILES - 3
    ROUNDS = (LAST_FULL - FIRST_FULL + 1) // 2

    x_t = x.rearrange("(t b) c n -> t (b c) n", b=2)
    out_t = out.rearrange("(t b) c n -> t (b c) n", b=2)
    ctx_t = ctx.rearrange("(t b) c m -> t (b c) m", b=2)
    A_v = A.rearrange("k (j r) d -> r k j d", r=RPC)
    B_v = B.rearrange("k d r -> k (d r)")

    with ExitStack() as stack:
        def sb(name, shape, dt=F32):
            return stack.enter_context(nc.sbuf_tensor(name, shape, dt))

        def bank(name):
            return stack.enter_context(nc.psum_tensor(name, [P, 512], F32))

        def sem(name):
            return stack.enter_context(nc.semaphore(name))

        wq = sb("wq", [C, C])
        wk2 = sb("wk2", [C, 2, C])
        wv2 = sb("wv2", [C, 2, C])
        ws2 = sb("ws2", [C, 2, C])
        wr = sb("wr", [K, D])
        a_raw = sb("a_raw", [P, KCH, D])
        b_raw = sb("b_raw", [P, DCH, P * RANK])
        gates_in = sb("gates_in", [P, 2])
        ident = sb("ident", [P, P])
        tanh_g = sb("tanh_g", [P, 2])
        qk_bd = sb("qk_bd", [P, P])
        wv_bd = sb("wv_bd", [P, P])
        ws_bd = sb("ws_bd", [P, P])
        ws_hi = sb("ws_hi", [P, P], F32R)
        ws_lo = sb("ws_lo", [P, P], F32R)
        a_hi = sb("a_hi", [P, DCH, K + KR], F32R)
        a_lo = sb("a_lo", [P, DCH, K + KR], F32R)
        b_hi = sb("b_hi", [P, KCH, D], F32R)
        b_lo = sb("b_lo", [P, KCH, D], F32R)
        minus_half = sb("minus_half", [P, 1])
        xt = [sb(f"xt{u}", [P, N]) for u in range(2)]
        ct = [sb(f"ct{u}", [P, M]) for u in range(2)]
        xn = sb("xn", [P, N])
        xn_hi = [sb(f"xn_hi{u}", [P, N], F32R) for u in range(2)]
        xn_lo = [sb(f"xn_lo{u}", [P, N], F32R) for u in range(2)]
        g_hi = [sb(f"g_hi{u}", [P, 2, M], F32R) for u in range(2)]
        g_lo = [sb(f"g_lo{u}", [P, 2, M], F32R) for u in range(2)]
        v_hi = [sb(f"v_hi{u}", [P, 2 * P], F32R) for u in range(2)]
        v_lo = [sb(f"v_lo{u}", [P, 2 * P], F32R) for u in range(2)]
        stats1 = sb("stats1", [P, 6])
        mean_var1 = sb("mean_var1", [P, 2])
        rstd1 = sb("rstd1", [P, 2])
        minus_max = sb("minus_max", [P, 2, 4])
        prob_sum = sb("prob_sum", [P, 2, 4])
        prob_rec = sb("prob_rec", [P, 2, 4])
        prob = sb("prob", [P, 2, 4, M])
        prob_n = sb("prob_n", [P, 2, 4, M])
        pt_hi = sb("pt_hi", [P, 2, N], F32R)
        pt_lo = sb("pt_lo", [P, 2, N], F32R)
        x1 = [sb(f"x1_{u}", [P, N]) for u in range(2)]
        stats2 = sb("stats2", [P, 6])
        mean_var2 = sb("mean_var2", [P, 2])
        rstd2 = sb("rstd2", [P, 2])
        xf = sb("xf", [P, N])
        xft_hi = sb("xft_hi", [P, NCH, P], F32R)
        xft_lo = sb("xft_lo", [P, NCH, P], F32R)
        scores = sb("scores", [P, K])
        scores_less8 = sb("scores_less8", [P, K])
        scores_less16 = sb("scores_less16", [P, K])
        top16 = sb("top16", [P, 2 * TOP])
        minus_top = sb("minus_top", [P, 1])
        gate_exp = sb("gate_exp", [P, K])
        gate = sb("gate", [P, K])
        gate_sum = sb("gate_sum", [P, 1])
        gate_rec = sb("gate_rec", [P, 1])
        out_scale = [sb(f"out_scale{u}", [P, 1]) for u in range(2)]
        hg = sb("hg", [P, KR])
        hgt_hi = sb("hgt_hi", [P, KCH, P], F32R)
        hgt_lo = sb("hgt_lo", [P, KCH, P], F32R)
        result = [sb(f"result{u}", [P, N]) for u in range(2)]

        ps_e = [bank("ps_e0"), bank("ps_e1")]
        ps_pt = bank("ps_pt")
        ps_yx = bank("ps_yx")
        ps_h = [bank("ps_h0"), bank("ps_h1"), bank("ps_h2")]
        ps_out = bank("ps_out")
        ps_gv = ps_h[2]

        wsmall_in, a_in, b_in = sem("wsmall_in"), sem("a_in"), sem("b_in")
        wr_in = sem("wr_in")
        x_in = [sem(f"x_in{u}") for u in range(2)]
        ctx_in = [sem(f"ctx_in{u}") for u in range(2)]
        stored = [sem(f"stored{u}") for u in range(2)]
        const_made = sem("const_made")
        tanh_made = sem("tanh_made")
        zeroed = sem("zeroed")
        wsmall_t = sem("wsmall_t")
        wr_t = sem("wr_t")
        a_t = sem("a_t")
        wsmall_ready = sem("wsmall_ready")
        ws_ready = sem("ws_ready")
        wr_hi_made = sem("wr_hi_made")
        wr_lo_made = sem("wr_lo_made")
        a_hi_made = sem("a_hi_made")
        a_lo_made = sem("a_lo_made")
        b_hi_made = sem("b_hi_made")
        b_lo_made = sem("b_lo_made")
        gv_made = sem("gv_made")
        e_made = sem("e_made")
        pt_made = sem("pt_made")
        y_made = sem("y_made")
        xft_made = sem("xft_made")
        h_made = sem("h_made")
        hgt_made = sem("hgt_made")
        out_made = sem("out_made")
        gv_hi_made = sem("gv_hi_made")
        xn_hi_made = sem("xn_hi_made")
        exp_made = sem("exp_made")
        pt_hi_made = sem("pt_hi_made")
        xft_hi_made = sem("xft_hi_made")
        gate_exp_made = sem("gate_exp_made")
        hgt_hi_made = sem("hgt_hi_made")
        ln1_step = sem("ln1_step")
        xn_made = sem("xn_made")
        gv_lo_made = sem("gv_lo_made")
        max_made = sem("max_made")
        rec_made = sem("rec_made")
        pt_lo_made = sem("pt_lo_made")
        x1_made = sem("x1_made")
        ln2_step = sem("ln2_step")
        xf_made = sem("xf_made")
        xft_lo_made = sem("xft_lo_made")
        top_step = sem("top_step")
        hg_made = sem("hg_made")
        hgt_lo_made = sem("hgt_lo_made")
        result_made = sem("result_made")
        rstd1_step = sem("rstd1_step")
        xn_lo_made = sem("xn_lo_made")
        norm_made = sem("norm_made")
        rstd2_step = sem("rstd2_step")

        def steps(engine, step):
            for i in range(-1, FIRST_FULL):
                step(Tile(i), 0 <= i + 1 < TILES, 0 <= i < TILES, 0 <= i - 1 < TILES, 0 <= i - 2 < TILES)
            with engine.Fori(0, ROUNDS) as rounds:
                for u in range(2):
                    step(Tile(FIRST_FULL + u, rounds), True, True, True, True)
            for i in range(LAST_FULL + 1, TILES + 2):
                step(Tile(i), 0 <= i + 1 < TILES, 0 <= i < TILES, 0 <= i - 1 < TILES, 0 <= i - 2 < TILES)

        block = stack.enter_context(nc.Block())

        @block.sync
        def _(sp):
            sp.dma_start(xt[0][:], x_t[0]).then_inc(x_in[0], 16)
            sp.dma_start(ct[0][:], ctx_t[0]).then_inc(ctx_in[0], 16)
            sp.dma_start(wq[:], Wq).then_inc(wsmall_in, 16)
            for w2, w in ((wk2, Wk), (wv2, Wv), (ws2, Wskip)):
                for b in range(2):
                    sp.dma_start(w2[:, b, :], w).then_inc(wsmall_in, 16)
            sp.dma_start(gates_in[:, 0:1], g_xattn.rearrange("(a n) -> a n", a=1).to_broadcast([P, 1])).then_inc(wsmall_in, 16)
            sp.dma_start(gates_in[:, 1:2], g_ffn.rearrange("(a n) -> a n", a=1).to_broadcast([P, 1])).then_inc(wsmall_in, 16)
            sp.dma_start(xt[1][:], x_t[1]).then_inc(x_in[1], 16)
            sp.dma_start(ct[1][:], ctx_t[1]).then_inc(ctx_in[1], 16)
            sp.dma_start(wr[:], Wr).then_inc(wr_in, 16)
            for r in range(RPC):
                sp.dma_start(a_raw[r * K:(r + 1) * K, :, :], A_v[r]).then_inc(a_in, 16)
            for c in range(DCH):
                for r in range(RPC):
                    width = P * RANK - r
                    sp.dma_start(b_raw[r * K:(r + 1) * K, c, 0:width],
                                 B_v[:, c * P * RANK + r:c * P * RANK + r + width]).then_inc(b_in, 16)

            def step(i, prep, attend, middle, last):
                if attend and (i.rounds is not None or i.number + 2 < TILES):
                    after(sp, gv_made, i.count(1, 1))
                    t2 = (i + 2).count(1)
                    sp.dma_start(ct[i.parity][:], ctx_t[t2]).then_inc(ctx_in[i.parity], 16)
                if last:
                    after(sp, result_made, (i + -2).count(1, 1))
                    sp.dma_start(out_t[(i + -2).count(1)], result[i.parity][:]).then_inc(stored[i.parity], 16)
                if attend and (i.rounds is not None or i.number + 2 < TILES):
                    after(sp, x1_made, i.count(1, 1))
                    sp.dma_start(xt[i.parity][:], x_t[t2]).then_inc(x_in[i.parity], 16)

            steps(sp, step)
            for u in range(2):
                sp.wait_ge(stored[u], 16 * (TILES // 2))

        @block.gpsimd
        def _(pool):
            nc.gpsimd.memset(ident[:], 0.0).then_inc(const_made, 1)
            nc.gpsimd.memset(minus_half[:], -0.5).then_inc(const_made, 1)
            pool.wait_ge(const_made, 1)
            nc.gpsimd.affine_select(out=ident[:], in_=ident[:], compare_op=ALU.not_equal, fill=1.0, base=0,
                                    pattern=[[-1, P]], channel_multiplier=1).then_inc(const_made, 1)
            b_view = b_raw[:].rearrange("p c (d j r) -> p c j d r", j=KCH, r=RPC)

            def split_b():
                for c in range(DCH):
                    pool.wait_ge(b_hi_made, c + 1)
                    nc.gpsimd.tensor_tensor(b_lo[:, :, c * P:(c + 1) * P], b_view[:, c, :, :, 0],
                                            b_hi[:, :, c * P:(c + 1) * P].bitcast(F32), ALU.subtract).then_inc(b_lo_made, 1)

            def step(i, prep, attend, middle, last):
                if attend:
                    for s in range(2):
                        after(pool, rec_made, i.count(2, s + 1))
                        nc.gpsimd.tensor_tensor(prob_n[:, s], prob[:, s],
                                                prob_rec[:, s, :].unsqueeze(2).to_broadcast([P, 4, M]), ALU.mult).then_inc(norm_made, 1)
                if prep:
                    p = i + 1
                    after_apart(pool, ln1_step, p.count(2, 2))
                    nc.gpsimd.tensor_scalar(rstd1[:, 1:2], mean_var1[:, 1:2], EPS, None, ALU.add).then_inc(rstd1_step, 1)
                    after(pool, rstd1_step, p.count(2, 1))
                    nc.gpsimd.tensor_tensor(rstd1[:, 0:1], rstd1[:, 1:2], minus_half[:], ALU.pow).then_inc(rstd1_step, 1)
                    after(pool, xn_hi_made, p.count(1, 1))
                    nc.gpsimd.tensor_tensor(xn_lo[p.parity][:], xn[:], xn_hi[p.parity][:].bitcast(F32), ALU.subtract).then_inc(xn_lo_made, 1)
                if attend:
                    after_apart(pool, ln2_step, i.count(2, 2))
                    nc.gpsimd.tensor_scalar(rstd2[:, 1:2], mean_var2[:, 1:2], EPS, None, ALU.add).then_inc(rstd2_step, 1)
                    after(pool, rstd2_step, i.count(2, 1))
                    nc.gpsimd.tensor_tensor(rstd2[:, 0:1], rstd2[:, 1:2], minus_half[:], ALU.pow).then_inc(rstd2_step, 1)
                if i.rounds is None and i.number == 0:
                    split_b()

            steps(pool, step)

        @block.scalar
        def _(act):
            act.wait_ge(wsmall_in, 16 * 9)
            nc.scalar.activation(tanh_g[:], gates_in[:], ACT.Tanh).then_inc(tanh_made, 1)
            act.wait_ge(wr_t, 1)
            nc.scalar.activation(a_hi[:, :, 0:K], ps_e[1][:, 0:DCH * K].rearrange("p (c k) -> p c k", c=DCH), ACT.Copy).then_inc(wr_hi_made, 1)

            def split_a():
                for g in range(2 * DCH):
                    c, half = g // 2, g % 2
                    act.wait_ge(a_t, g + 1)
                    lo = K + half * 512
                    nc.scalar.activation(a_hi[:, c, lo:lo + 512], (ps_h + [ps_out])[g % 4][:], ACT.Copy).then_inc(a_hi_made, 1)

            b_view = b_raw[:].rearrange("p c (d j r) -> p c j d r", j=KCH, r=RPC)

            def split_b():
                act.wait_ge(b_in, 16 * 2 * DCH)
                for c in range(DCH):
                    nc.scalar.activation(b_hi[:, :, c * P:(c + 1) * P], b_view[:, c, :, :, 0], ACT.Copy).then_inc(b_hi_made, 1)

            split_a()
            act.wait_ge(zeroed, 8)

            def step(i, prep, attend, middle, last):
                def exps(s):
                    after(act, max_made, i.count(2, s + 1))
                    after(act, norm_made, i.count(2, s - 1))
                    for q in range(4):
                        e = nc.scalar.activation(prob[:, s, q], ps_e[s][:, q * M:(q + 1) * M], ACT.Exp,
                                                 bias=minus_max[:, s, q:q + 1], accum_out=prob_sum[:, s, q:q + 1])
                    e.then_inc(exp_made, 1)

                def hgt_half(s):
                    after(act, hgt_made, (i + -2).count(2, s + 1))
                    nc.scalar.activation(hgt_hi[:, 4 * s:4 * s + 4], ps_h[s][:].rearrange("p (c t) -> p c t", c=4), ACT.Copy).then_inc(hgt_hi_made, 1)

                def pt_half(s):
                    after(act, pt_made, i.count(2, s + 1))
                    nc.scalar.activation(pt_hi[:, :, s * 256:(s + 1) * 256], ps_pt[:].rearrange("p (b n) -> p b n", b=2), ACT.Copy).then_inc(pt_hi_made, 1)

                if attend:
                    exps(0)
                if last:
                    hgt_half(0)
                if attend:
                    exps(1)
                if last:
                    hgt_half(1)
                if prep:
                    p = i + 1
                    u = p.parity
                    after(act, gv_made, p.count(1, 1))
                    for b in range(2):
                        nc.scalar.activation(g_hi[u][b * C:(b + 1) * C, b, :], ps_gv[b * C:(b + 1) * C, 0:M], ACT.Copy)
                    nc.scalar.activation(v_hi[u][:, 0:C], ps_gv[:, P:P + C], ACT.Copy)
                    nc.scalar.activation(v_hi[u][:, P + C:2 * P], ps_gv[:, P + C:2 * P], ACT.Copy).then_inc(gv_hi_made, 1)
                if attend:
                    pt_half(0)
                if middle:
                    after(act, xft_made, (i + -1).count(1, 1))
                    nc.scalar.activation(xft_hi[:].rearrange("p c t -> p (c t)"), ps_yx[:], ACT.Copy).then_inc(xft_hi_made, 1)
                if prep:
                    after(act, xn_made, p.count(1, 1))
                    nc.scalar.activation(xn_hi[u][:], xn[:], ACT.Copy).then_inc(xn_hi_made, 1)
                if attend:
                    pt_half(1)
                if middle:
                    after(act, top_step, (i + -1).count(9, 5))
                    nc.scalar.activation(gate_exp[:], scores[:], ACT.Exp, bias=minus_top[:]).then_inc(gate_exp_made, 1)
                if i.rounds is None and i.number == 0:
                    split_b()

            steps(act, step)

        @block.vector
        def _(dve):
            for u in range(2):
                nc.vector.memset(g_hi[u][:].bitcast(F32), 0.0).then_inc(zeroed, 1)
                nc.vector.memset(g_lo[u][:].bitcast(F32), 0.0).then_inc(zeroed, 1)
                nc.vector.memset(v_hi[u][:].bitcast(F32), 0.0).then_inc(zeroed, 1)
                nc.vector.memset(v_lo[u][:].bitcast(F32), 0.0).then_inc(zeroed, 1)
            nc.vector.memset(qk_bd[:], 0.0).then_inc(zeroed, 1)
            nc.vector.memset(wv_bd[:], 0.0).then_inc(zeroed, 1)
            nc.vector.memset(ws_bd[:], 0.0).then_inc(zeroed, 1)
            dve.wait_ge(zeroed, 11)
            dve.wait_ge(wsmall_t, 1)
            dve.wait_ge(tanh_made, 1)
            for b in range(2):
                rows, cols = slice(b * C, (b + 1) * C), slice(b * C, (b + 1) * C)
                nc.vector.tensor_scalar(qk_bd[rows, cols], ps_e[0][rows, 0:C], float(C) ** -0.5, None, ALU.mult).then_inc(wsmall_ready, 1)
                nc.vector.tensor_scalar(wv_bd[rows, cols], ps_e[0][rows, C:2 * C], tanh_g[rows, 0:1], None, ALU.mult).then_inc(wsmall_ready, 1)
                nc.vector.tensor_scalar(ws_bd[rows, cols], ps_e[0][rows, 2 * C:3 * C], tanh_g[rows, 0:1], None, ALU.mult).then_inc(wsmall_ready, 1)
            dve.wait_ge(wsmall_ready, 6)
            nc.vector.tensor_copy(ws_hi[:], ws_bd[:]).then_inc(ws_ready, 1)
            dve.wait_ge(ws_ready, 1)
            nc.vector.tensor_tensor(ws_lo[:], ws_bd[:], ws_hi[:].bitcast(F32), ALU.subtract).then_inc(ws_ready, 1)
            dve.wait_ge(wr_hi_made, 1)
            nc.vector.tensor_tensor(a_lo[:, :, 0:K], ps_e[1][:, 0:DCH * K].rearrange("p (c k) -> p c k", c=DCH),
                                    a_hi[:, :, 0:K].bitcast(F32), ALU.subtract).then_inc(wr_lo_made, 1)
            for g in range(2 * DCH):
                c, half = g // 2, g % 2
                dve.wait_ge(a_hi_made, g + 1)
                lo = K + half * 512
                nc.vector.tensor_tensor(a_lo[:, c, lo:lo + 512], (ps_h + [ps_out])[g % 4][:],
                                        a_hi[:, c, lo:lo + 512].bitcast(F32), ALU.subtract).then_inc(a_lo_made, 1)

            def step(i, prep, attend, middle, last):
                p, f, o = i + 1, i + -1, i + -2

                def gate_bank(t, s):
                    first, end = H_BLOCKS[s]
                    skip = 1 if s == 0 else 0
                    after(dve, h_made, t.count(3, s + 1))
                    after(dve, hgt_made, t.count(2, -1 if s == 0 else 0))
                    after(dve, top_step, t.count(9, 7))
                    n = end - first - skip
                    nc.vector.tensor_tensor(hg[:, (first + skip - 1) * K:(end - 1) * K].rearrange("p (r k) -> p r k", k=K),
                                            ps_h[s][:, skip * K:(end - first) * K].rearrange("p (r k) -> p r k", k=K),
                                            gate[:].unsqueeze(1).to_broadcast([P, n, K]), ALU.mult).then_inc(hg_made, 1)

                def hgt_half(s):
                    after(dve, hgt_hi_made, o.count(2, s + 1))
                    nc.vector.tensor_tensor(hgt_lo[:, 4 * s:4 * s + 4], ps_h[s][:].rearrange("p (c t) -> p c t", c=4),
                                            hgt_hi[:, 4 * s:4 * s + 4].bitcast(F32), ALU.subtract).then_inc(hgt_lo_made, 1)

                def largest(s):
                    after(dve, e_made, i.count(2, s + 1))
                    nc.vector.tensor_reduce(minus_max[:, s, :], ps_e[s][:].rearrange("p (q m) -> p q m", q=4),
                                            axis=AX_X, op=ALU.max, negate=True).then_inc(max_made, 1)

                def reciprocals(s):
                    after(dve, exp_made, i.count(2, s + 1))
                    nc.vector.reciprocal(prob_rec[:, s, :], prob_sum[:, s, :]).then_inc(rec_made, 1)

                def pt_half(s):
                    after(dve, pt_hi_made, i.count(2, s + 1))
                    half = slice(s * 256, (s + 1) * 256)
                    nc.vector.tensor_tensor(pt_lo[:, :, half], ps_pt[:].rearrange("p (b n) -> p b n", b=2),
                                            pt_hi[:, :, half].bitcast(F32), ALU.subtract).then_inc(pt_lo_made, 1)

                if last:
                    gate_bank(o, 2)
                if attend:
                    largest(0)
                    largest(1)
                if last:
                    hgt_half(0)
                if attend:
                    reciprocals(0)
                if last:
                    hgt_half(1)
                if attend:
                    reciprocals(1)
                if prep:
                    u = p.parity
                    after(dve, gv_hi_made, p.count(1, 1))
                    for b in range(2):
                        nc.vector.tensor_tensor(g_lo[u][b * C:(b + 1) * C, b, :], ps_gv[b * C:(b + 1) * C, 0:M],
                                                g_hi[u][b * C:(b + 1) * C, b, :].bitcast(F32), ALU.subtract)
                    nc.vector.tensor_tensor(v_lo[u][:, 0:C], ps_gv[:, P:P + C], v_hi[u][:, 0:C].bitcast(F32), ALU.subtract)
                    nc.vector.tensor_tensor(v_lo[u][:, P + C:2 * P], ps_gv[:, P + C:2 * P],
                                            v_hi[u][:, P + C:2 * P].bitcast(F32), ALU.subtract).then_inc(gv_lo_made, 1)
                    after(dve, x_in[u], p.dma_count(1))
                    nc.vector.bn_stats(stats1[:], xt[u][:]).then_inc(ln1_step, 1)
                    after_apart(dve, ln1_step, p.count(2, 1))
                    nc.vector.bn_aggr(mean_var1[:], stats1[:]).then_inc(ln1_step, 1)
                if attend:
                    pt_half(0)
                if middle:
                    after(dve, xft_hi_made, f.count(1, 1))
                    nc.vector.tensor_tensor(xft_lo[:].rearrange("p c t -> p (c t)"), ps_yx[:],
                                            xft_hi[:].rearrange("p c t -> p (c t)").bitcast(F32), ALU.subtract).then_inc(xft_lo_made, 1)
                if prep:
                    after(dve, rstd1_step, p.count(2, 2))
                    after(dve, ln1_step, p.count(2, 2))
                    after(dve, xn_lo_made, p.count(1))
                    nc.vector.tensor_scalar(xn[:], xt[u][:], mean_var1[:, 0:1], rstd1[:, 0:1], ALU.subtract, ALU.mult).then_inc(xn_made, 1)
                if attend:
                    pt_half(1)
                if last:
                    after(dve, out_made, o.count(1, 1))
                    after(dve, stored[i.parity], o.dma_count())
                    after(dve, top_step, o.count(9, 9))
                    nc.vector.scalar_tensor_tensor(result[i.parity][:], ps_out[:], out_scale[i.parity][:], x1[i.parity][:],
                                                   ALU.mult, ALU.add).then_inc(result_made, 1)
                if middle:
                    after(dve, h_made, f.count(3, 1))
                    nc.vector.tensor_copy(scores[:], ps_h[0][:, 0:K]).then_inc(top_step, 1)
                    after_apart(dve, top_step, f.count(9, 1))
                    nc.vector.max(top16[:, 0:TOP], scores[:]).then_inc(top_step, 1)
                    after_apart(dve, top_step, f.count(9, 2))
                    nc.vector.match_replace(scores_less8[:], top16[:, 0:TOP], scores[:], REPLACED).then_inc(top_step, 1)
                    after_apart(dve, top_step, f.count(9, 3))
                    nc.vector.max(top16[:, TOP:2 * TOP], scores_less8[:]).then_inc(top_step, 1)
                    nc.vector.tensor_scalar(minus_top[:], top16[:, 0:1], -1.0, None, ALU.mult).then_inc(top_step, 1)
                    after_apart(dve, top_step, f.count(9, 5))
                    nc.vector.match_replace(scores_less16[:], top16[:, TOP:2 * TOP], scores_less8[:], REPLACED).then_inc(top_step, 1)
                    after(dve, top_step, f.count(9, 6))
                    after(dve, gate_exp_made, f.count(1, 1))
                    nc.vector.scalar_tensor_tensor(gate[:], scores_less16[:], REPLACED, gate_exp[:], ALU.is_le, ALU.mult,
                                                   accum_out=gate_sum[:]).then_inc(top_step, 1)
                    after(dve, top_step, f.count(9, 7))
                    nc.vector.reciprocal(gate_rec[:], gate_sum[:]).then_inc(top_step, 1)
                    after(dve, top_step, f.count(9, 8))
                    nc.vector.tensor_scalar(out_scale[f.parity][:], gate_rec[:], tanh_g[:, 1:2], FFN_SCALING,
                                            ALU.mult, ALU.mult).then_inc(top_step, 1)
                    gate_bank(f, 0)
                if attend:
                    after(dve, y_made, i.count(1, 1))
                    nc.vector.tensor_tensor(x1[i.parity][:], ps_yx[:], xt[i.parity][:], ALU.add).then_inc(x1_made, 1)
                    after(dve, x1_made, i.count(1, 1))
                    nc.vector.bn_stats(stats2[:], x1[i.parity][:]).then_inc(ln2_step, 1)
                    after_apart(dve, ln2_step, i.count(2, 1))
                    nc.vector.bn_aggr(mean_var2[:], stats2[:]).then_inc(ln2_step, 1)
                if middle:
                    gate_bank(f, 1)
                if attend:
                    after(dve, rstd2_step, i.count(2, 2))
                    after(dve, ln2_step, i.count(2, 2))
                    nc.vector.tensor_scalar(xf[:], x1[i.parity][:], mean_var2[:, 0:1], rstd2[:, 0:1], ALU.subtract, ALU.mult).then_inc(xf_made, 1)

            steps(dve, step)

        @block.tensor
        def _(pe):
            pe.wait_ge(const_made, 3)
            pe.wait_ge(wsmall_in, 16 * 9)
            flat = "o b c -> o (b c)"
            nc.tensor.matmul(ps_e[0][:, 0:C], wk2[:].rearrange(flat), wq[:], start=True, stop=True)
            nc.tensor.transpose(ps_e[0][:, C:2 * C], wv2[:].rearrange(flat), ident[0:C, 0:C])
            nc.tensor.transpose(ps_e[0][:, 2 * C:3 * C], ws2[:].rearrange(flat), ident[0:C, 0:C]).then_inc(wsmall_t, 1)
            pe.wait_ge(wr_in, 16)
            for c in range(DCH):
                w = nc.tensor.transpose(ps_e[1][:, c * K:(c + 1) * K], wr[:, c * P:(c + 1) * P], ident[0:K, 0:K])
            w.then_inc(wr_t, 1)
            pe.wait_ge(a_in, 16 * RPC)
            for g in range(2 * DCH):
                c, half = g // 2, g % 2
                if g >= 4:
                    pe.wait_ge(a_lo_made, g - 3)
                for j in range(4):
                    w = nc.tensor.transpose((ps_h + [ps_out])[g % 4][:, j * P:(j + 1) * P],
                                            a_raw[:, 4 * half + j, c * P:(c + 1) * P], ident[:])
                w.then_inc(a_t, 1)
            pe.wait_ge(a_lo_made, 2 * DCH)
            pe.wait_ge(wr_lo_made, 1)
            pe.wait_ge(wsmall_ready, 6)
            pe.wait_ge(ws_ready, 2)
            pe.wait_ge(zeroed, 11)

            def split_product(dst, hi_l, lo_l, hi_r, lo_r, start, stop):
                nc.tensor.matmul(dst, hi_l, hi_r, start=start, stop=False)
                nc.tensor.matmul(dst, hi_l, lo_r, start=False, stop=False)
                return nc.tensor.matmul(dst, lo_l, hi_r, start=False, stop=stop)

            def step(i, prep, attend, middle, last):
                p, f, o = i + 1, i + -1, i + -2
                u = i.parity

                def energies(s):
                    after(pe, exp_made, i.count(2, s - 1))
                    for q in range(2):
                        n = (2 * s + q) * P
                        w = split_product(ps_e[s][:, q * 2 * M:(q + 1) * 2 * M],
                                          xn_hi[u][:, n:n + P], xn_lo[u][:, n:n + P],
                                          g_hi[u][:].rearrange("p b m -> p (b m)"), g_lo[u][:].rearrange("p b m -> p (b m)"),
                                          True, True)
                    w.then_inc(e_made, 1)

                def prob_transposes(s):
                    after(pe, norm_made, i.count(2, s + 1))
                    after(pe, pt_lo_made, i.count(2, s))
                    for q in range(2):
                        for b in range(2):
                            w = nc.tensor.transpose(ps_pt[:, b * 256 + q * P:b * 256 + (q + 1) * P], prob_n[:, s, 2 * q + b, :], ident[:])
                    w.then_inc(pt_made, 1)

                def hg_transposes(s):
                    after(pe, hg_made, o.count(3, 2 + s))
                    for j in range(4):
                        w = nc.tensor.transpose(ps_h[s][:, j * P:(j + 1) * P], hg[:, (4 * s + j) * P:(4 * s + j + 1) * P], ident[:])
                    w.then_inc(hgt_made, 1)

                def out_half(s):
                    after(pe, hgt_lo_made, o.count(2, s + 1))
                    for j in range(4 * s, 4 * s + 4):
                        w = split_product(ps_out[:], hgt_hi[:, j], hgt_lo[:, j], b_hi[:, j], b_lo[:, j], j == 0, j == KCH - 1)
                    return w

                def h_bank(s):
                    first, end = H_BLOCKS[s]
                    cols = slice(first * K, end * K)
                    for c in range(DCH):
                        w = split_product(ps_h[s][:, 0:(end - first) * K], xft_hi[:, c], xft_lo[:, c],
                                          a_hi[:, c, cols], a_lo[:, c, cols], c == 0, c == DCH - 1)
                    w.then_inc(h_made, 1)

                if attend:
                    after(pe, xn_lo_made, i.count(1, 1))
                    after(pe, gv_lo_made, i.count(1, 1))
                    energies(0)
                    energies(1)
                if last:
                    hg_transposes(0)
                    hg_transposes(1)
                if prep:
                    after(pe, ctx_in[p.parity], p.dma_count(1))
                    after(pe, gv_lo_made, p.count(1))
                    nc.tensor.matmul(ps_gv[:, 0:M], qk_bd[:], ct[p.parity][:], start=True, stop=True)
                    nc.tensor.matmul(ps_gv[:, P:2 * P], ct[p.parity][:], wv_bd[:], start=True, stop=True).then_inc(gv_made, 1)
                if last:
                    if o.rounds is None and o.number == 0:
                        pe.wait_ge(b_lo_made, DCH)
                    after(pe, result_made, o.count(1))
                    out_half(0)
                if attend:
                    prob_transposes(0)
                if middle:
                    after(pe, xf_made, f.count(1, 1))
                    for c in range(NCH):
                        w = nc.tensor.transpose(ps_yx[:, c * P:(c + 1) * P], xf[:, c * P:(c + 1) * P], ident[:])
                    w.then_inc(xft_made, 1)
                if last:
                    out_half(1).then_inc(out_made, 1)
                if attend:
                    prob_transposes(1)
                if middle:
                    after(pe, xft_lo_made, f.count(1, 1))
                    after(pe, hgt_lo_made, f.count(2, -1))
                    h_bank(0)
                if attend:
                    after(pe, xft_lo_made, i.count(1))
                    split_product(ps_yx[:], ws_hi[:], ws_lo[:], xn_hi[u][:], xn_lo[u][:], True, False)
                    after(pe, pt_lo_made, i.count(2, 2))
                    for b in range(2):
                        half = slice(b * P, (b + 1) * P)
                        w = split_product(ps_yx[:], v_hi[u][:, half], v_lo[u][:, half], pt_hi[:, b], pt_lo[:, b], False, b == 1)
                    w.then_inc(y_made, 1)
                if middle:
                    after(pe, hgt_lo_made, f.count(2, 0))
                    h_bank(1)
                    if prep:
                        after(pe, gv_lo_made, p.count(1, 1))
                    h_bank(2)

            steps(pe, step)


INPUTS = ["x", "ctx_1024", "g_xattn", "g_ffn", "L0_xattn_Wq", "L0_xattn_Wk", "L0_xattn_Wv", "L0_xattn_Wskip",
          "L0_ffn_A", "L0_ffn_B", "L0_ffn_Wr"]


def kernel(**inputs):
    import numpy as np
    import concourse.bacc as bacc
    from concourse.bass_utils import run_bass_kernel_spmd

    nc = bacc.Bacc("TRN2", target_bir_lowering=False, num_devices=1)
    arrays, args = {}, []
    for name in INPUTS:
        a = np.ascontiguousarray(inputs[name])
        arrays[f"in_{name}"] = a
        args.append(nc.dram_tensor(f"in_{name}", a.shape, mybir.dt.from_np(a.dtype), kind="ExternalInput").ap())
    out = nc.dram_tensor("out_x", arrays["in_x"].shape, F32, kind="ExternalOutput").ap()
    flamingo_block(nc, *args, out)
    r = run_bass_kernel_spmd(nc, [arrays], core_ids=[0])
    return r.results[0]["out_x"]
```

```python
from contextlib import ExitStack

import concourse.bass as bass
from concourse import mybir

F32 = mybir.dt.float32
F32R = mybir.dt.float32r
ALU = mybir.AluOpType
ACT = mybir.ActivationFunctionType
AX_X = mybir.AxisListType.X

P = 128
EPS = 1e-5
REPLACED = -3.0e38
FFN_SCALING = 32.0 / 16


class Tile:

    def __init__(self, number, rounds=None):
        self.number, self.rounds = number, rounds

    def __add__(self, k):
        return Tile(self.number + k, self.rounds)

    @property
    def parity(self):
        return self.number % 2

    def count(self, per_tile, more=0):
        fixed = per_tile * self.number + more
        return fixed if self.rounds is None else self.rounds * (2 * per_tile) + fixed

    def dma_count(self, more=0):
        fixed = 16 * (self.number // 2 + more)
        return fixed if self.rounds is None else self.rounds * 16 + fixed


def after(engine, semaphore, value):
    if not isinstance(value, int) or value > 0:
        engine.wait_ge(semaphore, value)


def after_apart(engine, semaphore, value):
    after(engine, semaphore, value)
    engine.nop(nofuse=True)


def flamingo_block(nc, x, ctx, g_xattn, g_ffn, Wq, Wk, Wv, Wskip, A, B, Wr, out):
    batches, C, N = x.shape
    M = ctx.shape[2]
    K, RANK, D = A.shape
    TILES = batches * C // P
    NCH = N // P
    DCH = D // P
    KR = K * RANK
    KCH = KR // P
    RPC = P // K
    TOP = 8
    H_BLOCKS = [(0, 6), (6, 12), (12, 17)]
    FIRST_FULL, LAST_FULL = 4, TILES - 3
    ROUNDS = (LAST_FULL - FIRST_FULL + 1) // 2

    x_t = x.rearrange("(t b) c n -> t (b c) n", b=2)
    out_t = out.rearrange("(t b) c n -> t (b c) n", b=2)
    ctx_t = ctx.rearrange("(t b) c m -> t (b c) m", b=2)
    A_v = A.rearrange("k (j r) d -> r k j d", r=RPC)
    B_v = B.rearrange("k d r -> k (d r)")

    with ExitStack() as stack:
        def sb(name, shape, dt=F32):
            return stack.enter_context(nc.sbuf_tensor(name, shape, dt))

        def bank(name):
            return stack.enter_context(nc.psum_tensor(name, [P, 512], F32))

        def sem(name):
            return stack.enter_context(nc.semaphore(name))

        wq = sb("wq", [C, C])
        wk2 = sb("wk2", [C, 2, C])
        wv2 = sb("wv2", [C, 2, C])
        ws2 = sb("ws2", [C, 2, C])
        wr = sb("wr", [K, D])
        a_raw = sb("a_raw", [P, KCH, D])
        b_raw = sb("b_raw", [P, DCH, P * RANK])
        gates_in = sb("gates_in", [P, 2])
        ident = sb("ident", [P, P])
        tanh_g = sb("tanh_g", [P, 2])
        qk_bd = sb("qk_bd", [P, P])
        wv_bd = sb("wv_bd", [P, P])
        ws_bd = sb("ws_bd", [P, P])
        ws_hi = sb("ws_hi", [P, P], F32R)
        ws_lo = sb("ws_lo", [P, P], F32R)
        a_hi = sb("a_hi", [P, DCH, K + KR], F32R)
        a_lo = sb("a_lo", [P, DCH, K + KR], F32R)
        b_hi = sb("b_hi", [P, KCH, D], F32R)
        b_lo = sb("b_lo", [P, KCH, D], F32R)
        minus_half = sb("minus_half", [P, 1])
        xt = [sb(f"xt{u}", [P, N]) for u in range(2)]
        ct = [sb(f"ct{u}", [P, M]) for u in range(2)]
        xn = sb("xn", [P, N])
        xn_hi = [sb(f"xn_hi{u}", [P, N], F32R) for u in range(2)]
        xn_lo = [sb(f"xn_lo{u}", [P, N], F32R) for u in range(2)]
        g_hi = [sb(f"g_hi{u}", [P, 2, M], F32R) for u in range(2)]
        g_lo = [sb(f"g_lo{u}", [P, 2, M], F32R) for u in range(2)]
        v_hi = [sb(f"v_hi{u}", [P, 2 * P], F32R) for u in range(2)]
        v_lo = [sb(f"v_lo{u}", [P, 2 * P], F32R) for u in range(2)]
        stats1 = sb("stats1", [P, 6])
        mean_var1 = sb("mean_var1", [P, 2])
        rstd1 = sb("rstd1", [P, 2])
        minus_max = sb("minus_max", [P, 2, 4])
        prob_sum = sb("prob_sum", [P, 2, 4])
        prob_rec = sb("prob_rec", [P, 2, 4])
        prob = sb("prob", [P, 2, 4, M])
        prob_n = sb("prob_n", [P, 2, 4, M])
        pt_hi = sb("pt_hi", [P, 2, N], F32R)
        pt_lo = sb("pt_lo", [P, 2, N], F32R)
        x1 = [sb(f"x1_{u}", [P, N]) for u in range(2)]
        stats2 = sb("stats2", [P, 6])
        mean_var2 = sb("mean_var2", [P, 2])
        rstd2 = sb("rstd2", [P, 2])
        xf = sb("xf", [P, N])
        xft_hi = sb("xft_hi", [P, NCH, P], F32R)
        xft_lo = sb("xft_lo", [P, NCH, P], F32R)
        scores = sb("scores", [P, K])
        scores_less8 = sb("scores_less8", [P, K])
        scores_less16 = sb("scores_less16", [P, K])
        top16 = sb("top16", [P, 2 * TOP])
        minus_top = sb("minus_top", [P, 1])
        gate_exp = sb("gate_exp", [P, K])
        gate = sb("gate", [P, K])
        gate_sum = sb("gate_sum", [P, 1])
        gate_rec = sb("gate_rec", [P, 1])
        out_scale = [sb(f"out_scale{u}", [P, 1]) for u in range(2)]
        hg = sb("hg", [P, KR])
        hgt_hi = sb("hgt_hi", [P, KCH, P], F32R)
        hgt_lo = sb("hgt_lo", [P, KCH, P], F32R)
        result = [sb(f"result{u}", [P, N]) for u in range(2)]

        ps_e = [bank("ps_e0"), bank("ps_e1")]
        ps_pt = bank("ps_pt")
        ps_yx = bank("ps_yx")
        ps_h = [bank("ps_h0"), bank("ps_h1"), bank("ps_h2")]
        ps_out = bank("ps_out")
        ps_gv = ps_h[2]

        qk_in = sem("qk_in")
        g_in = sem("g_in")
        vs_in = sem("vs_in")
        wr_in = sem("wr_in")
        a_in = sem("a_in")
        b_in = [sem(f"b_in{c}") for c in range(DCH)]
        x_in = [sem(f"x_in{u}") for u in range(2)]
        ctx_in = [sem(f"ctx_in{u}") for u in range(2)]
        stored = [sem(f"stored{u}") for u in range(2)]
        const_made = sem("const_made")
        tanh_made = sem("tanh_made")
        zeroed = sem("zeroed")
        qk_t = sem("qk_t")
        vs_t = sem("vs_t")
        a_t = sem("a_t")
        qkv_ready = sem("qkv_ready")
        ws_ready = sem("ws_ready")
        wr_hi_made = sem("wr_hi_made")
        wr_lo_made = sem("wr_lo_made")
        a_hi_made = sem("a_hi_made")
        a_lo_made = sem("a_lo_made")
        b_hi_made = sem("b_hi_made")
        b_lo_made = sem("b_lo_made")
        gv_made = sem("gv_made")
        e_made = sem("e_made")
        pt_made = sem("pt_made")
        y_made = sem("y_made")
        xft_made = sem("xft_made")
        h_made = sem("h_made")
        hgt_made = sem("hgt_made")
        out_made = sem("out_made")
        gv_hi_made = sem("gv_hi_made")
        xn_hi_made = sem("xn_hi_made")
        exp_made = sem("exp_made")
        pt_hi_made = sem("pt_hi_made")
        xft_hi_made = sem("xft_hi_made")
        gate_exp_made = sem("gate_exp_made")
        hgt_hi_made = sem("hgt_hi_made")
        ln1_step = sem("ln1_step")
        xn_made = sem("xn_made")
        gv_lo_made = sem("gv_lo_made")
        max_made = sem("max_made")
        rec_made = sem("rec_made")
        pt_lo_made = sem("pt_lo_made")
        x1_made = sem("x1_made")
        ln2_step = sem("ln2_step")
        xf_made = sem("xf_made")
        xft_lo_made = sem("xft_lo_made")
        top_step = sem("top_step")
        hg_made = sem("hg_made")
        hgt_lo_made = sem("hgt_lo_made")
        result_made = sem("result_made")
        rstd1_step = sem("rstd1_step")
        xn_lo_made = sem("xn_lo_made")
        norm_made = sem("norm_made")
        rstd2_step = sem("rstd2_step")

        def steps(engine, step):
            for i in range(FIRST_FULL):
                step(Tile(i), 0 <= i + 1 < TILES, 0 <= i < TILES, 0 <= i - 1 < TILES, 0 <= i - 2 < TILES)
            with engine.Fori(0, ROUNDS) as rounds:
                for u in range(2):
                    step(Tile(FIRST_FULL + u, rounds), True, True, True, True)
            for i in range(LAST_FULL + 1, TILES + 2):
                step(Tile(i), 0 <= i + 1 < TILES, 0 <= i < TILES, 0 <= i - 1 < TILES, 0 <= i - 2 < TILES)

        def is_step(i, number):
            return i.rounds is None and i.number == number

        a_banks = [ps_h[0], ps_h[1], ps_out]
        A_GROUPS = 2 * DCH
        b_view = b_raw[:].rearrange("p c (d j r) -> p c j d r", j=KCH, r=RPC)

        def a_group(g):
            return g // 2, K + g % 2 * 512

        block = stack.enter_context(nc.Block())

        @block.sync
        def _(sp):
            def load_b(c):
                for r in range(RPC):
                    width = P * RANK - r
                    sp.dma_start(b_raw[r * K:(r + 1) * K, c, 0:width],
                                 B_v[:, c * P * RANK + r:c * P * RANK + r + width]).then_inc(b_in[c], 16)

            sp.dma_start(xt[0][:], x_t[0]).then_inc(x_in[0], 16)
            sp.dma_start(wq[:], Wq).then_inc(qk_in, 16)
            sp.dma_start(wk2[:], Wk.unsqueeze(1).to_broadcast([C, 2, C])).then_inc(qk_in, 16)
            sp.dma_start(wv2[:], Wv.unsqueeze(1).to_broadcast([C, 2, C])).then_inc(vs_in, 16)
            sp.dma_start(ct[0][:], ctx_t[0]).then_inc(ctx_in[0], 16)
            sp.dma_start(ws2[:], Wskip.unsqueeze(1).to_broadcast([C, 2, C])).then_inc(vs_in, 16)
            sp.dma_start(wr[:], Wr).then_inc(wr_in, 16)
            sp.dma_start(xt[1][:], x_t[1]).then_inc(x_in[1], 16)
            sp.dma_start(ct[1][:], ctx_t[1]).then_inc(ctx_in[1], 16)
            for r in range(RPC):
                sp.dma_start(a_raw[r * K:(r + 1) * K, :, :], A_v[r]).then_inc(a_in, 16)
            load_b(0)
            load_b(1)

            def step(i, prep, attend, middle, last):
                if attend and (i.rounds is not None or i.number + 2 < TILES):
                    after(sp, gv_made, i.count(1, 1))
                    t2 = (i + 2).count(1)
                    sp.dma_start(ct[i.parity][:], ctx_t[t2]).then_inc(ctx_in[i.parity], 16)
                if last:
                    after(sp, result_made, (i + -2).count(1, 1))
                    sp.dma_start(out_t[(i + -2).count(1)], result[i.parity][:]).then_inc(stored[i.parity], 16)
                if attend and (i.rounds is not None or i.number + 2 < TILES):
                    after(sp, x1_made, i.count(1, 1))
                    sp.dma_start(xt[i.parity][:], x_t[t2]).then_inc(x_in[i.parity], 16)
                if is_step(i, 0):
                    load_b(2)
                    load_b(3)

            steps(sp, step)
            for u in range(2):
                sp.wait_ge(stored[u], 16 * (TILES // 2))

        @block.gpsimd
        def _(pool):
            nc.gpsimd.memset(ident[:], 0.0).then_inc(const_made, 1)
            nc.gpsimd.memset(minus_half[:], -0.5).then_inc(const_made, 1)
            pool.wait_ge(const_made, 1)
            nc.gpsimd.affine_select(out=ident[:], in_=ident[:], compare_op=ALU.not_equal, fill=1.0, base=0,
                                    pattern=[[-1, P]], channel_multiplier=1).then_inc(const_made, 1)
            def prepare(p):
                after_apart(pool, ln1_step, p.count(2, 2))
                nc.gpsimd.tensor_scalar(rstd1[:, 1:2], mean_var1[:, 1:2], EPS, None, ALU.add).then_inc(rstd1_step, 1)
                after(pool, rstd1_step, p.count(2, 1))
                nc.gpsimd.tensor_tensor(rstd1[:, 0:1], rstd1[:, 1:2], minus_half[:], ALU.pow).then_inc(rstd1_step, 1)
                after(pool, xn_hi_made, p.count(1, 1))
                nc.gpsimd.tensor_tensor(xn_lo[p.parity][:], xn[:], xn_hi[p.parity][:].bitcast(F32), ALU.subtract).then_inc(xn_lo_made, 1)

            prepare(Tile(0))

            def step(i, prep, attend, middle, last):
                if attend:
                    for s in range(2):
                        after(pool, rec_made, i.count(2, s + 1))
                        nc.gpsimd.tensor_tensor(prob_n[:, s], prob[:, s],
                                                prob_rec[:, s, :].unsqueeze(2).to_broadcast([P, 4, M]), ALU.mult).then_inc(norm_made, 1)
                if prep:
                    prepare(i + 1)
                if attend:
                    after_apart(pool, ln2_step, i.count(2, 2))
                    nc.gpsimd.tensor_scalar(rstd2[:, 1:2], mean_var2[:, 1:2], EPS, None, ALU.add).then_inc(rstd2_step, 1)
                    after(pool, rstd2_step, i.count(2, 1))
                    nc.gpsimd.tensor_tensor(rstd2[:, 0:1], rstd2[:, 1:2], minus_half[:], ALU.pow).then_inc(rstd2_step, 1)

            steps(pool, step)

        @block.scalar
        def _(act):
            for n, g in enumerate((g_xattn, g_ffn)):
                act.dma_start(gates_in[:, n:n + 1], g.rearrange("(a n) -> a n", a=1).to_broadcast([P, 1])).then_inc(g_in, 16)
            act.wait_ge(g_in, 32)
            nc.scalar.activation(tanh_g[:], gates_in[:], ACT.Tanh).then_inc(tanh_made, 1)

            def split_a(groups):
                for g in groups:
                    c, col = a_group(g)
                    act.wait_ge(a_t, g + 1)
                    nc.scalar.activation(a_hi[:, c, col:col + 512], a_banks[g % 3][:], ACT.Copy).then_inc(a_hi_made, 1)

            def split_b(c):
                act.wait_ge(b_in[c], 16 * RPC)
                nc.scalar.activation(b_hi[:, :, c * P:(c + 1) * P], b_view[:, c, :, :, 0], ACT.Copy).then_inc(b_hi_made, 1)

            def split_xn(p):
                after(act, xn_made, p.count(1, 1))
                nc.scalar.activation(xn_hi[p.parity][:], xn[:], ACT.Copy).then_inc(xn_hi_made, 1)

            def split_gv(p):
                u = p.parity
                after(act, gv_made, p.count(1, 1))
                for b in range(2):
                    nc.scalar.activation(g_hi[u][b * C:(b + 1) * C, b, :], ps_gv[b * C:(b + 1) * C, 0:M], ACT.Copy)
                nc.scalar.activation(v_hi[u][:, 0:C], ps_gv[:, P:P + C], ACT.Copy)
                nc.scalar.activation(v_hi[u][:, P + C:2 * P], ps_gv[:, P + C:2 * P], ACT.Copy).then_inc(gv_hi_made, 1)

            split_xn(Tile(0))
            act.wait_ge(zeroed, 8)
            split_gv(Tile(0))
            act.wait_ge(vs_t, 1)
            act.wait_ge(ws_ready, 2)
            nc.scalar.activation(a_hi[:, :, 0:K], ps_e[1][:, 0:DCH * K].rearrange("p (c k) -> p c k", c=DCH), ACT.Copy).then_inc(wr_hi_made, 1)

            def step(i, prep, attend, middle, last):
                def exps(s):
                    after(act, max_made, i.count(2, s + 1))
                    after(act, norm_made, i.count(2, s - 1))
                    for q in range(4):
                        e = nc.scalar.activation(prob[:, s, q], ps_e[s][:, q * M:(q + 1) * M], ACT.Exp,
                                                 bias=minus_max[:, s, q:q + 1], accum_out=prob_sum[:, s, q:q + 1])
                    e.then_inc(exp_made, 1)

                def hgt_half(s):
                    after(act, hgt_made, (i + -2).count(2, s + 1))
                    nc.scalar.activation(hgt_hi[:, 4 * s:4 * s + 4], ps_h[s][:].rearrange("p (c t) -> p c t", c=4), ACT.Copy).then_inc(hgt_hi_made, 1)

                def pt_half(s):
                    after(act, pt_made, i.count(2, s + 1))
                    nc.scalar.activation(pt_hi[:, :, s * 256:(s + 1) * 256], ps_pt[:].rearrange("p (b n) -> p b n", b=2), ACT.Copy).then_inc(pt_hi_made, 1)

                def xft():
                    after(act, xft_made, (i + -1).count(1, 1))
                    nc.scalar.activation(xft_hi[:].rearrange("p c t -> p (c t)"), ps_yx[:], ACT.Copy).then_inc(xft_hi_made, 1)

                if is_step(i, 1):
                    xft()
                if last:
                    hgt_half(0)
                if attend:
                    exps(0)
                if last:
                    hgt_half(1)
                if attend:
                    exps(1)
                if is_step(i, 0):
                    split_a(range(0, 2))
                if prep:
                    split_gv(i + 1)
                if is_step(i, 0):
                    split_a(range(2, 4))
                if attend:
                    pt_half(0)
                if middle and not is_step(i, 1):
                    xft()
                if is_step(i, 1):
                    split_b(0)
                if prep:
                    split_xn(i + 1)
                if is_step(i, 0):
                    split_a(range(4, 6))
                if attend:
                    pt_half(1)
                if is_step(i, 0):
                    split_a(range(6, 8))
                if middle:
                    after(act, top_step, (i + -1).count(9, 5))
                    nc.scalar.activation(gate_exp[:], scores[:], ACT.Exp, bias=minus_top[:]).then_inc(gate_exp_made, 1)
                if is_step(i, 1):
                    for c in range(1, DCH):
                        split_b(c)

            steps(act, step)

        @block.vector
        def _(dve):
            for u in range(2):
                nc.vector.memset(g_hi[u][:].bitcast(F32), 0.0).then_inc(zeroed, 1)
                nc.vector.memset(g_lo[u][:].bitcast(F32), 0.0).then_inc(zeroed, 1)
                nc.vector.memset(v_hi[u][:].bitcast(F32), 0.0).then_inc(zeroed, 1)
                nc.vector.memset(v_lo[u][:].bitcast(F32), 0.0).then_inc(zeroed, 1)
            nc.vector.memset(qk_bd[:], 0.0).then_inc(zeroed, 1)
            nc.vector.memset(wv_bd[:], 0.0).then_inc(zeroed, 1)
            nc.vector.memset(ws_bd[:], 0.0).then_inc(zeroed, 1)

            def split_a(groups):
                for g in groups:
                    c, col = a_group(g)
                    dve.wait_ge(a_hi_made, g + 1)
                    nc.vector.tensor_tensor(a_lo[:, c, col:col + 512], a_banks[g % 3][:],
                                            a_hi[:, c, col:col + 512].bitcast(F32), ALU.subtract).then_inc(a_lo_made, 1)

            def split_b(c):
                dve.wait_ge(b_hi_made, c + 1)
                nc.vector.tensor_tensor(b_lo[:, :, c * P:(c + 1) * P], b_view[:, c, :, :, 0],
                                        b_hi[:, :, c * P:(c + 1) * P].bitcast(F32), ALU.subtract).then_inc(b_lo_made, 1)

            def split_gv(p):
                u = p.parity
                after(dve, gv_hi_made, p.count(1, 1))
                for b in range(2):
                    nc.vector.tensor_tensor(g_lo[u][b * C:(b + 1) * C, b, :], ps_gv[b * C:(b + 1) * C, 0:M],
                                            g_hi[u][b * C:(b + 1) * C, b, :].bitcast(F32), ALU.subtract)
                nc.vector.tensor_tensor(v_lo[u][:, 0:C], ps_gv[:, P:P + C], v_hi[u][:, 0:C].bitcast(F32), ALU.subtract)
                nc.vector.tensor_tensor(v_lo[u][:, P + C:2 * P], ps_gv[:, P + C:2 * P],
                                        v_hi[u][:, P + C:2 * P].bitcast(F32), ALU.subtract).then_inc(gv_lo_made, 1)

            def statistics(p):
                after(dve, x_in[p.parity], p.dma_count(1))
                nc.vector.bn_stats(stats1[:], xt[p.parity][:]).then_inc(ln1_step, 1)
                after_apart(dve, ln1_step, p.count(2, 1))
                nc.vector.bn_aggr(mean_var1[:], stats1[:]).then_inc(ln1_step, 1)

            def normalize(p):
                after(dve, rstd1_step, p.count(2, 2))
                after(dve, ln1_step, p.count(2, 2))
                after(dve, xn_lo_made, p.count(1))
                nc.vector.tensor_scalar(xn[:], xt[p.parity][:], mean_var1[:, 0:1], rstd1[:, 0:1], ALU.subtract, ALU.mult).then_inc(xn_made, 1)

            statistics(Tile(0))
            dve.wait_ge(zeroed, 11)
            dve.wait_ge(qk_t, 1)
            for b in range(2):
                own = slice(b * C, (b + 1) * C)
                nc.vector.tensor_scalar(qk_bd[own, own], ps_e[0][own, 0:C], float(C) ** -0.5, None, ALU.mult).then_inc(qkv_ready, 1)
            normalize(Tile(0))
            dve.wait_ge(tanh_made, 1)
            dve.wait_ge(vs_t, 1)
            for b in range(2):
                own = slice(b * C, (b + 1) * C)
                nc.vector.tensor_scalar(wv_bd[own, own], ps_e[1][own, DCH * K:DCH * K + C], tanh_g[own, 0:1], None, ALU.mult).then_inc(qkv_ready, 1)
            for b in range(2):
                own = slice(b * C, (b + 1) * C)
                nc.vector.tensor_scalar(ws_bd[own, own], ps_e[1][own, DCH * K + C:DCH * K + 2 * C], tanh_g[own, 0:1], None, ALU.mult).then_inc(ws_ready, 1)
            dve.wait_ge(ws_ready, 2)
            nc.vector.tensor_copy(ws_hi[:], ws_bd[:]).then_inc(ws_ready, 1)
            dve.wait_ge(ws_ready, 3)
            nc.vector.tensor_tensor(ws_lo[:], ws_bd[:], ws_hi[:].bitcast(F32), ALU.subtract).then_inc(ws_ready, 1)
            split_gv(Tile(0))
            dve.wait_ge(wr_hi_made, 1)
            nc.vector.tensor_tensor(a_lo[:, :, 0:K], ps_e[1][:, 0:DCH * K].rearrange("p (c k) -> p c k", c=DCH),
                                    a_hi[:, :, 0:K].bitcast(F32), ALU.subtract).then_inc(wr_lo_made, 1)

            def step(i, prep, attend, middle, last):
                p, f, o = i + 1, i + -1, i + -2

                def gate_bank(t, s):
                    first, end = H_BLOCKS[s]
                    skip = 1 if s == 0 else 0
                    after(dve, h_made, t.count(3, s + 1))
                    after(dve, hgt_made, t.count(2, -1 if s == 0 else 0))
                    after(dve, top_step, t.count(9, 7))
                    n = end - first - skip
                    nc.vector.tensor_tensor(hg[:, (first + skip - 1) * K:(end - 1) * K].rearrange("p (r k) -> p r k", k=K),
                                            ps_h[s][:, skip * K:(end - first) * K].rearrange("p (r k) -> p r k", k=K),
                                            gate[:].unsqueeze(1).to_broadcast([P, n, K]), ALU.mult).then_inc(hg_made, 1)

                def hgt_half(s):
                    after(dve, hgt_hi_made, o.count(2, s + 1))
                    nc.vector.tensor_tensor(hgt_lo[:, 4 * s:4 * s + 4], ps_h[s][:].rearrange("p (c t) -> p c t", c=4),
                                            hgt_hi[:, 4 * s:4 * s + 4].bitcast(F32), ALU.subtract).then_inc(hgt_lo_made, 1)

                def largest(s):
                    after(dve, e_made, i.count(2, s + 1))
                    nc.vector.tensor_reduce(minus_max[:, s, :], ps_e[s][:].rearrange("p (q m) -> p q m", q=4),
                                            axis=AX_X, op=ALU.max, negate=True).then_inc(max_made, 1)

                def reciprocals(s):
                    after(dve, exp_made, i.count(2, s + 1))
                    nc.vector.reciprocal(prob_rec[:, s, :], prob_sum[:, s, :]).then_inc(rec_made, 1)

                def pt_half(s):
                    after(dve, pt_hi_made, i.count(2, s + 1))
                    half = slice(s * 256, (s + 1) * 256)
                    nc.vector.tensor_tensor(pt_lo[:, :, half], ps_pt[:].rearrange("p (b n) -> p b n", b=2),
                                            pt_hi[:, :, half].bitcast(F32), ALU.subtract).then_inc(pt_lo_made, 1)

                def xft():
                    after(dve, xft_hi_made, f.count(1, 1))
                    nc.vector.tensor_tensor(xft_lo[:].rearrange("p c t -> p (c t)"), ps_yx[:],
                                            xft_hi[:].rearrange("p c t -> p (c t)").bitcast(F32), ALU.subtract).then_inc(xft_lo_made, 1)

                if is_step(i, 1):
                    xft()
                if last:
                    gate_bank(o, 2)
                if attend:
                    largest(0)
                if last:
                    hgt_half(0)
                if attend:
                    largest(1)
                    reciprocals(0)
                if last:
                    hgt_half(1)
                if attend:
                    reciprocals(1)
                if is_step(i, 0):
                    split_a(range(0, 2))
                if prep:
                    split_gv(p)
                    statistics(p)
                if is_step(i, 0):
                    split_a(range(2, 4))
                if attend:
                    pt_half(0)
                if middle and not is_step(i, 1):
                    xft()
                if is_step(i, 1):
                    split_b(0)
                if prep:
                    normalize(p)
                if is_step(i, 0):
                    split_a(range(4, 6))
                if attend:
                    pt_half(1)
                if is_step(i, 0):
                    split_a(range(6, 8))
                if last:
                    after(dve, out_made, o.count(1, 1))
                    after(dve, stored[i.parity], o.dma_count())
                    after(dve, top_step, o.count(9, 9))
                    nc.vector.scalar_tensor_tensor(result[i.parity][:], ps_out[:], out_scale[i.parity][:], x1[i.parity][:],
                                                   ALU.mult, ALU.add).then_inc(result_made, 1)
                if middle:
                    after(dve, h_made, f.count(3, 1))
                    nc.vector.tensor_copy(scores[:], ps_h[0][:, 0:K]).then_inc(top_step, 1)
                    after_apart(dve, top_step, f.count(9, 1))
                    nc.vector.max(top16[:, 0:TOP], scores[:]).then_inc(top_step, 1)
                    after_apart(dve, top_step, f.count(9, 2))
                    nc.vector.match_replace(scores_less8[:], top16[:, 0:TOP], scores[:], REPLACED).then_inc(top_step, 1)
                    after_apart(dve, top_step, f.count(9, 3))
                    nc.vector.max(top16[:, TOP:2 * TOP], scores_less8[:]).then_inc(top_step, 1)
                    nc.vector.tensor_scalar(minus_top[:], top16[:, 0:1], -1.0, None, ALU.mult).then_inc(top_step, 1)
                    after_apart(dve, top_step, f.count(9, 5))
                    nc.vector.match_replace(scores_less16[:], top16[:, TOP:2 * TOP], scores_less8[:], REPLACED).then_inc(top_step, 1)
                    after(dve, top_step, f.count(9, 6))
                    after(dve, gate_exp_made, f.count(1, 1))
                    nc.vector.scalar_tensor_tensor(gate[:], scores_less16[:], REPLACED, gate_exp[:], ALU.is_le, ALU.mult,
                                                   accum_out=gate_sum[:]).then_inc(top_step, 1)
                    after(dve, top_step, f.count(9, 7))
                    nc.vector.reciprocal(gate_rec[:], gate_sum[:]).then_inc(top_step, 1)
                    after(dve, top_step, f.count(9, 8))
                    nc.vector.tensor_scalar(out_scale[f.parity][:], gate_rec[:], tanh_g[:, 1:2], FFN_SCALING,
                                            ALU.mult, ALU.mult).then_inc(top_step, 1)
                    gate_bank(f, 0)
                if attend:
                    after(dve, y_made, i.count(1, 1))
                    nc.vector.tensor_tensor(x1[i.parity][:], ps_yx[:], xt[i.parity][:], ALU.add).then_inc(x1_made, 1)
                    after(dve, x1_made, i.count(1, 1))
                    nc.vector.bn_stats(stats2[:], x1[i.parity][:]).then_inc(ln2_step, 1)
                    after_apart(dve, ln2_step, i.count(2, 1))
                    nc.vector.bn_aggr(mean_var2[:], stats2[:]).then_inc(ln2_step, 1)
                if middle:
                    gate_bank(f, 1)
                if attend:
                    after(dve, rstd2_step, i.count(2, 2))
                    after(dve, ln2_step, i.count(2, 2))
                    nc.vector.tensor_scalar(xf[:], x1[i.parity][:], mean_var2[:, 0:1], rstd2[:, 0:1], ALU.subtract, ALU.mult).then_inc(xf_made, 1)
                if is_step(i, 1):
                    for c in range(1, DCH):
                        split_b(c)

            steps(dve, step)

        @block.tensor
        def _(pe):
            pe.wait_ge(const_made, 3)
            flat = "o b c -> o (b c)"
            pe.wait_ge(qk_in, 32)
            nc.tensor.matmul(ps_e[0][:, 0:C], wk2[:].rearrange(flat), wq[:], start=True, stop=True).then_inc(qk_t, 1)
            pe.wait_ge(vs_in, 32)
            nc.tensor.transpose(ps_e[1][:, DCH * K:DCH * K + C], wv2[:].rearrange(flat), ident[0:C, 0:C])
            nc.tensor.transpose(ps_e[1][:, DCH * K + C:DCH * K + 2 * C], ws2[:].rearrange(flat), ident[0:C, 0:C])
            pe.wait_ge(wr_in, 16)
            for c in range(DCH):
                w = nc.tensor.transpose(ps_e[1][:, c * K:(c + 1) * K], wr[:, c * P:(c + 1) * P], ident[0:K, 0:K])
            w.then_inc(vs_t, 1)

            def a_transposes(groups):
                pe.wait_ge(a_in, 16 * RPC)
                for g in groups:
                    if g >= 3:
                        pe.wait_ge(a_lo_made, g - 2)
                    for j in range(4):
                        w = nc.tensor.transpose(a_banks[g % 3][:, j * P:(j + 1) * P],
                                                a_raw[:, g % 2 * 4 + j, g // 2 * P:(g // 2 + 1) * P], ident[:])
                    w.then_inc(a_t, 1)

            def context_products(p):
                after(pe, ctx_in[p.parity], p.dma_count(1))
                after(pe, gv_lo_made, p.count(1))
                nc.tensor.matmul(ps_gv[:, 0:M], qk_bd[:], ct[p.parity][:], start=True, stop=True)
                nc.tensor.matmul(ps_gv[:, P:2 * P], ct[p.parity][:], wv_bd[:], start=True, stop=True).then_inc(gv_made, 1)

            pe.wait_ge(zeroed, 11)
            pe.wait_ge(qkv_ready, 4)
            context_products(Tile(0))
            pe.wait_ge(wr_lo_made, 1)
            pe.wait_ge(ws_ready, 4)

            def split_product(dst, hi_l, lo_l, hi_r, lo_r, start, stop):
                nc.tensor.matmul(dst, hi_l, hi_r, start=start, stop=False)
                nc.tensor.matmul(dst, hi_l, lo_r, start=False, stop=False)
                return nc.tensor.matmul(dst, lo_l, hi_r, start=False, stop=stop)

            def step(i, prep, attend, middle, last):
                p, f, o = i + 1, i + -1, i + -2
                u = i.parity

                def energies(s):
                    after(pe, exp_made, i.count(2, s - 1))
                    for q in range(2):
                        n = (2 * s + q) * P
                        w = split_product(ps_e[s][:, q * 2 * M:(q + 1) * 2 * M],
                                          xn_hi[u][:, n:n + P], xn_lo[u][:, n:n + P],
                                          g_hi[u][:].rearrange("p b m -> p (b m)"), g_lo[u][:].rearrange("p b m -> p (b m)"),
                                          True, True)
                    w.then_inc(e_made, 1)

                def prob_transposes(s):
                    after(pe, norm_made, i.count(2, s + 1))
                    after(pe, pt_lo_made, i.count(2, s))
                    for q in range(2):
                        for b in range(2):
                            w = nc.tensor.transpose(ps_pt[:, b * 256 + q * P:b * 256 + (q + 1) * P], prob_n[:, s, 2 * q + b, :], ident[:])
                    w.then_inc(pt_made, 1)

                def hg_transposes(s):
                    after(pe, hg_made, o.count(3, 2 + s))
                    for j in range(4):
                        w = nc.tensor.transpose(ps_h[s][:, j * P:(j + 1) * P], hg[:, (4 * s + j) * P:(4 * s + j + 1) * P], ident[:])
                    w.then_inc(hgt_made, 1)

                def out_half(s):
                    after(pe, hgt_lo_made, o.count(2, s + 1))
                    for j in range(4 * s, 4 * s + 4):
                        w = split_product(ps_out[:], hgt_hi[:, j], hgt_lo[:, j], b_hi[:, j], b_lo[:, j], j == 0, j == KCH - 1)
                    return w

                def h_bank(s):
                    first, end = H_BLOCKS[s]
                    cols = slice(first * K, end * K)
                    for c in range(DCH):
                        w = split_product(ps_h[s][:, 0:(end - first) * K], xft_hi[:, c], xft_lo[:, c],
                                          a_hi[:, c, cols], a_lo[:, c, cols], c == 0, c == DCH - 1)
                    w.then_inc(h_made, 1)

                def xf_transposes():
                    after(pe, xf_made, f.count(1, 1))
                    for c in range(NCH):
                        w = nc.tensor.transpose(ps_yx[:, c * P:(c + 1) * P], xf[:, c * P:(c + 1) * P], ident[:])
                    w.then_inc(xft_made, 1)

                def first_h_bank():
                    after(pe, xft_lo_made, f.count(1, 1))
                    after(pe, hgt_lo_made, f.count(2, -1))
                    h_bank(0)

                if last:
                    hg_transposes(0)
                if is_step(i, 1):
                    xf_transposes()
                if attend:
                    after(pe, xn_lo_made, i.count(1, 1))
                    after(pe, gv_lo_made, i.count(1, 1))
                    energies(0)
                    energies(1)
                if last:
                    hg_transposes(1)
                if is_step(i, 0):
                    a_transposes(range(0, 2))
                if prep:
                    context_products(p)
                if is_step(i, 0):
                    a_transposes(range(2, 4))
                if is_step(i, 1):
                    pe.wait_ge(a_lo_made, A_GROUPS)
                    first_h_bank()
                if last:
                    if is_step(i, 2):
                        pe.wait_ge(b_lo_made, DCH)
                    after(pe, result_made, o.count(1))
                    out_half(0)
                if attend:
                    prob_transposes(0)
                if is_step(i, 0):
                    a_transposes(range(4, 6))
                if middle and not is_step(i, 1):
                    xf_transposes()
                if last:
                    out_half(1).then_inc(out_made, 1)
                if attend:
                    prob_transposes(1)
                if is_step(i, 0):
                    a_transposes(range(6, 8))
                if middle and not is_step(i, 1):
                    first_h_bank()
                if attend:
                    after(pe, xft_lo_made, i.count(1))
                    split_product(ps_yx[:], ws_hi[:], ws_lo[:], xn_hi[u][:], xn_lo[u][:], True, False)
                    after(pe, pt_lo_made, i.count(2, 2))
                    for b in range(2):
                        half = slice(b * P, (b + 1) * P)
                        w = split_product(ps_yx[:], v_hi[u][:, half], v_lo[u][:, half], pt_hi[:, b], pt_lo[:, b], False, b == 1)
                    w.then_inc(y_made, 1)
                if middle:
                    after(pe, hgt_lo_made, f.count(2, 0))
                    h_bank(1)
                    if prep:
                        after(pe, gv_lo_made, p.count(1, 1))
                    h_bank(2)

            steps(pe, step)


INPUTS = ["x", "ctx_1024", "g_xattn", "g_ffn", "L0_xattn_Wq", "L0_xattn_Wk", "L0_xattn_Wv", "L0_xattn_Wskip",
          "L0_ffn_A", "L0_ffn_B", "L0_ffn_Wr"]


def kernel(**inputs):
    import numpy as np
    import concourse.bacc as bacc
    from concourse.bass_utils import run_bass_kernel_spmd

    nc = bacc.Bacc("TRN2", target_bir_lowering=False, num_devices=1)
    arrays, args = {}, []
    for name in INPUTS:
        a = np.ascontiguousarray(inputs[name])
        arrays[f"in_{name}"] = a
        args.append(nc.dram_tensor(f"in_{name}", a.shape, mybir.dt.from_np(a.dtype), kind="ExternalInput").ap())
    out = nc.dram_tensor("out_x", arrays["in_x"].shape, F32, kind="ExternalOutput").ap()
    flamingo_block(nc, *args, out)
    r = run_bass_kernel_spmd(nc, [arrays], core_ids=[0])
    return r.results[0]["out_x"]
```

```python
from contextlib import ExitStack

import concourse.bass as bass
from concourse import mybir

F32 = mybir.dt.float32
F32R = mybir.dt.float32r
ALU = mybir.AluOpType
ACT = mybir.ActivationFunctionType
AX_X = mybir.AxisListType.X

P = 128
EPS = 1e-5
REPLACED = -3.0e38
FFN_SCALING = 32.0 / 16


class Tile:

    def __init__(self, number, rounds=None):
        self.number, self.rounds = number, rounds

    def __add__(self, k):
        return Tile(self.number + k, self.rounds)

    @property
    def parity(self):
        return self.number % 2

    def count(self, per_tile, more=0):
        fixed = per_tile * self.number + more
        return fixed if self.rounds is None else self.rounds * (2 * per_tile) + fixed

    def pair_count(self, per_pair, more=0):
        fixed = per_pair * (self.number // 2) + more
        return fixed if self.rounds is None else self.rounds * per_pair + fixed

    def dma_count(self, more=0):
        return self.pair_count(16, 16 * more)


def after(engine, semaphore, value):
    if not isinstance(value, int) or value > 0:
        engine.wait_ge(semaphore, value)


def after_apart(engine, semaphore, value):
    after(engine, semaphore, value)
    engine.nop(nofuse=True)


def flamingo_block(nc, x, ctx, g_xattn, g_ffn, Wq, Wk, Wv, Wskip, A, B, Wr, out):
    batches, C, N = x.shape
    M = ctx.shape[2]
    K, RANK, D = A.shape
    TILES = batches * C // P
    NCH = N // P
    DCH = D // P
    KR = K * RANK
    KCH = KR // P
    RPC = P // K
    TOP = 8
    FIRST_ROWS = 2 * P
    GROUPS = 3
    FIRST_FULL, LAST_FULL = 4, TILES - 2
    RAMP = 3
    ROUNDS = (LAST_FULL - FIRST_FULL + 1) // 2

    x_t = x.rearrange("(t b) c n -> t (b c) n", b=2)
    out_t = out.rearrange("(t b) c n -> t (b c) n", b=2)
    ctx_t = ctx.rearrange("(t b) c m -> t (b c) m", b=2)
    A_v = A.rearrange("k (j r) d -> r k j d", r=RPC)
    B_v = B.rearrange("k d r -> k (d r)")

    with ExitStack() as stack:
        def sb(name, shape, dt=F32):
            return stack.enter_context(nc.sbuf_tensor(name, shape, dt))

        def bank(name):
            return stack.enter_context(nc.psum_tensor(name, [P, 512], F32))

        def sem(name):
            return stack.enter_context(nc.semaphore(name))

        wq = sb("wq", [C, C])
        wk2 = sb("wk2", [C, 2, C])
        wv2 = sb("wv2", [C, 2, C])
        ws2 = sb("ws2", [C, 2, C])
        wr = sb("wr", [K, D])
        a_raw = sb("a_raw", [P, KCH, D])
        b_raw = sb("b_raw", [P, DCH, P * RANK])
        gates_in = sb("gates_in", [P, 2])
        ident = sb("ident", [P, P])
        tanh_g = sb("tanh_g", [P, 2])
        gate_factor = sb("gate_factor", [P, 1])
        qk_bd = sb("qk_bd", [P, P])
        wv_bd = sb("wv_bd", [P, P])
        ws_bd = sb("ws_bd", [P, P])
        ws_hi = sb("ws_hi", [P, P], F32R)
        ws_lo = sb("ws_lo", [P, P], F32R)
        a_hi = sb("a_hi", [P, DCH, K + KR], F32R)
        a_lo = sb("a_lo", [P, DCH, K + KR], F32R)
        b_hi = sb("b_hi", [P, KCH, D], F32R)
        b_lo = sb("b_lo", [P, KCH, D], F32R)
        minus_half = sb("minus_half", [P, 1])
        xt = [sb(f"xt{u}", [P, N]) for u in range(2)]
        ct = [sb(f"ct{u}", [P, M]) for u in range(2)]
        xn = sb("xn", [P, N])
        xn_hi = [sb(f"xn_hi{u}", [P, N], F32R) for u in range(2)]
        xn_lo = [sb(f"xn_lo{u}", [P, N], F32R) for u in range(2)]
        g_hi = [sb(f"g_hi{u}", [P, 2, M], F32R) for u in range(2)]
        g_lo = [sb(f"g_lo{u}", [P, 2, M], F32R) for u in range(2)]
        v_hi = [sb(f"v_hi{u}", [P, 2 * P], F32R) for u in range(2)]
        v_lo = [sb(f"v_lo{u}", [P, 2 * P], F32R) for u in range(2)]
        stats1 = sb("stats1", [P, 6])
        mean_var1 = sb("mean_var1", [P, 2])
        rstd1 = sb("rstd1", [P, 2])
        minus_max = sb("minus_max", [P, 2, 4])
        prob_sum = sb("prob_sum", [P, 2, 4])
        prob_rec = sb("prob_rec", [P, 2, 4])
        prob = sb("prob", [P, 2, 4, M])
        prob_n = sb("prob_n", [P, 2, 4, M])
        pt_hi = sb("pt_hi", [P, 2, N], F32R)
        pt_lo = sb("pt_lo", [P, 2, N], F32R)
        x1 = [sb(f"x1_{u}", [P, N]) for u in range(2)]
        x1_held = [sb(f"x1_held{u}", [P, N]) for u in range(2)]
        stats2 = sb("stats2", [P, 6])
        mean_var2 = sb("mean_var2", [P, 2])
        rstd2 = sb("rstd2", [P, 2])
        xf = sb("xf", [P, N])
        xft_hi = sb("xft_hi", [P, NCH, 2 * P], F32R)
        xft_lo = sb("xft_lo", [P, NCH, 2 * P], F32R)
        scores = sb("scores", [P, K])
        scores_less8 = sb("scores_less8", [P, K])
        scores_less16 = sb("scores_less16", [P, K])
        top16 = sb("top16", [P, 2 * TOP])
        minus_top = sb("minus_top", [P, 1])
        gate_exp = sb("gate_exp", [P, K])
        gate = sb("gate", [P, K])
        gate_sum = sb("gate_sum", [P, 1])
        gate_rec = sb("gate_rec", [P, 1])
        gates = sb("gates", [P, 2, K])
        gates_t = sb("gates_t", [P, 2 * P])
        hg_first = sb("hg_first", [P, FIRST_ROWS])
        hg = sb("hg", [P, 2, 4 * P])
        hgt_hi = sb("hgt_hi", [P, KCH, 2 * P], F32R)
        hgt_lo = sb("hgt_lo", [P, KCH, 2 * P], F32R)
        result = [sb(f"result{u}", [P, N]) for u in range(2)]

        ps_e = [bank("ps_e0"), bank("ps_e1")]
        ps_pt = bank("ps_pt")
        ps_yx = bank("ps_yx")
        ps_gv = bank("ps_gv")
        ps_s = bank("ps_s")
        ps_h0 = bank("ps_h0")
        ps_out = bank("ps_out")
        ps_h = [ps_h0, ps_out, ps_h0]
        v_blocks = "p (q c) -> p q c"

        qk_in = sem("qk_in")
        g_in = sem("g_in")
        vs_in = sem("vs_in")
        wr_in = sem("wr_in")
        a_in = sem("a_in")
        b_in = [sem(f"b_in{c}") for c in range(DCH)]
        x_in = [sem(f"x_in{u}") for u in range(2)]
        ctx_in = [sem(f"ctx_in{u}") for u in range(2)]
        stored = sem("stored")
        const_made = sem("const_made")
        tanh_made = sem("tanh_made")
        factor_made = sem("factor_made")
        zeroed = sem("zeroed")
        qk_t = sem("qk_t")
        vs_t = sem("vs_t")
        wr_t = sem("wr_t")
        a_t = sem("a_t")
        qk_ready = sem("qk_ready")
        wv_ready = sem("wv_ready")
        ws_ready = sem("ws_ready")
        wr_hi_made = sem("wr_hi_made")
        wr_lo_made = sem("wr_lo_made")
        a_hi_made = sem("a_hi_made")
        a_lo_made = sem("a_lo_made")
        b_hi_made = sem("b_hi_made")
        b_lo_made = sem("b_lo_made")
        g_made = sem("g_made")
        v_made = sem("v_made")
        e_made = sem("e_made")
        pt_made = sem("pt_made")
        y_made = sem("y_made")
        xf_turned = sem("xf_turned")
        scores_made = sem("scores_made")
        gates_turned = sem("gates_turned")
        h_made = sem("h_made")
        out_made = sem("out_made")
        g_hi_made = sem("g_hi_made")
        v_hi_made = sem("v_hi_made")
        xn_hi_made = sem("xn_hi_made")
        exp_made = sem("exp_made")
        pt_hi_made = sem("pt_hi_made")
        xft_hi_made = sem("xft_hi_made")
        gate_exp_made = sem("gate_exp_made")
        hgt_hi_made = sem("hgt_hi_made")
        first_hi_made = sem("first_hi_made")
        gates_t_made = sem("gates_t_made")
        held = sem("held")
        ln1_step = sem("ln1_step")
        xn_made = sem("xn_made")
        g_lo_made = sem("g_lo_made")
        v_lo_made = sem("v_lo_made")
        max_made = sem("max_made")
        rec_made = sem("rec_made")
        pt_lo_made = sem("pt_lo_made")
        x1_made = sem("x1_made")
        ln2_step = sem("ln2_step")
        xf_made = sem("xf_made")
        xft_lo_made = sem("xft_lo_made")
        top_step = sem("top_step")
        hg_first_made = sem("hg_first_made")
        hg_made = sem("hg_made")
        hgt_lo_made = sem("hgt_lo_made")
        first_lo_made = sem("first_lo_made")
        result_made = sem("result_made")
        rstd1_step = sem("rstd1_step")
        xn_lo_made = sem("xn_lo_made")
        norm_made = sem("norm_made")
        rstd2_step = sem("rstd2_step")

        def stages(number):
            return (number + 1 < TILES,) + tuple(0 <= number - back < TILES for back in range(4))

        def steps(engine, step):
            for i in range(RAMP, FIRST_FULL):
                step(Tile(i), *stages(i))
            with engine.Fori(0, ROUNDS) as rounds:
                for u in range(2):
                    step(Tile(FIRST_FULL + u, rounds), True, True, True, True, True)
            for i in range(FIRST_FULL + 2 * ROUNDS, TILES + 3):
                step(Tile(i), *stages(i))

        a_banks = [ps_s, ps_out, ps_h0, ps_s, ps_out, ps_h0, ps_out, ps_h0]
        A_GROUPS = 2 * DCH
        b_view = b_raw[:].rearrange("p c (d j r) -> p c j d r", j=KCH, r=RPC)

        def a_group(g):
            return g % DCH, g // DCH

        block = stack.enter_context(nc.Block())

        @block.sync
        def _(sp):
            def load_b(c):
                for r in range(RPC):
                    width = P * RANK - r
                    sp.dma_start(b_raw[r * K:(r + 1) * K, c, 0:width],
                                 B_v[:, c * P * RANK + r:c * P * RANK + r + width]).then_inc(b_in[c], 16)

            sp.dma_start(xt[0][:], x_t[0]).then_inc(x_in[0], 16)
            sp.dma_start(ct[0][:], ctx_t[0]).then_inc(ctx_in[0], 16)
            sp.dma_start(wv2[:], Wv.unsqueeze(1).to_broadcast([C, 2, C])).then_inc(vs_in, 16)
            sp.dma_start(ws2[:], Wskip.unsqueeze(1).to_broadcast([C, 2, C])).then_inc(vs_in, 16)
            sp.dma_start(wr[:], Wr).then_inc(wr_in, 16)
            sp.dma_start(xt[1][:], x_t[1]).then_inc(x_in[1], 16)
            sp.dma_start(ct[1][:], ctx_t[1]).then_inc(ctx_in[1], 16)
            for r in range(RPC):
                sp.dma_start(a_raw[r * K:(r + 1) * K, :, :], A_v[r]).then_inc(a_in, 16)
            for c in range(DCH):
                load_b(c)

            def step(i, prep, attend, route, second, third):
                o = i + -3
                if attend and (i.rounds is not None or i.number + 2 < TILES):
                    after(sp, v_made, i.count(1, 1))
                    t2 = (i + 2).count(1)
                    sp.dma_start(ct[i.parity][:], ctx_t[t2]).then_inc(ctx_in[i.parity], 16)
                if third:
                    after(sp, result_made, o.count(1, 1))
                    sp.dma_start(out_t[o.count(1)], result[o.parity][:]).then_inc(stored, 16)
                if attend and (i.rounds is not None or i.number + 2 < TILES):
                    after(sp, x1_made, i.count(1, 1))
                    sp.dma_start(xt[i.parity][:], x_t[t2]).then_inc(x_in[i.parity], 16)

            for i in range(RAMP):
                step(Tile(i), *stages(i))
            steps(sp, step)
            sp.wait_ge(stored, 16 * TILES)

        @block.gpsimd
        def _(pool):
            nc.gpsimd.memset(ident[:], 0.0).then_inc(const_made, 1)
            nc.gpsimd.memset(minus_half[:], -0.5).then_inc(const_made, 1)
            pool.wait_ge(const_made, 1)
            nc.gpsimd.affine_select(out=ident[:], in_=ident[:], compare_op=ALU.not_equal, fill=1.0, base=0,
                                    pattern=[[-1, P]], channel_multiplier=1).then_inc(const_made, 1)

            def split_b(c):
                pool.wait_ge(b_hi_made, c + 1)
                nc.gpsimd.tensor_tensor(b_lo[:, :, c * P:(c + 1) * P], b_view[:, c, :, :, 0],
                                        b_hi[:, :, c * P:(c + 1) * P].bitcast(F32), ALU.subtract).then_inc(b_lo_made, 1)

            def inverse_deviation(p):
                after_apart(pool, ln1_step, p.count(2, 2))
                nc.gpsimd.tensor_scalar(rstd1[:, 1:2], mean_var1[:, 1:2], EPS, None, ALU.add).then_inc(rstd1_step, 1)
                after(pool, rstd1_step, p.count(2, 1))
                nc.gpsimd.tensor_tensor(rstd1[:, 0:1], rstd1[:, 1:2], minus_half[:], ALU.pow).then_inc(rstd1_step, 1)

            def split_xn(p):
                after(pool, xn_hi_made, p.count(1, 1))
                nc.gpsimd.tensor_tensor(xn_lo[p.parity][:], xn[:], xn_hi[p.parity][:].bitcast(F32), ALU.subtract).then_inc(xn_lo_made, 1)

            def divide(t, s):
                after(pool, rec_made, t.count(2, s + 1))
                after(pool, pt_made, t.count(2, s - 1))
                nc.gpsimd.tensor_tensor(prob_n[:, s], prob[:, s],
                                        prob_rec[:, s, :].unsqueeze(2).to_broadcast([P, 4, M]), ALU.mult).then_inc(norm_made, 1)

            def inverse_deviation_x1(t):
                after_apart(pool, ln2_step, t.count(2, 2))
                nc.gpsimd.tensor_scalar(rstd2[:, 1:2], mean_var2[:, 1:2], EPS, None, ALU.add).then_inc(rstd2_step, 1)
                after(pool, rstd2_step, t.count(2, 1))
                nc.gpsimd.tensor_tensor(rstd2[:, 0:1], rstd2[:, 1:2], minus_half[:], ALU.pow).then_inc(rstd2_step, 1)

            def ramp():
                inverse_deviation(Tile(0))
                inverse_deviation(Tile(1))
                split_xn(Tile(1))
                for t in range(2):
                    divide(Tile(t), 0)
                    divide(Tile(t), 1)
                inverse_deviation_x1(Tile(0))
                split_b(0)
                inverse_deviation(Tile(2))
                split_xn(Tile(2))
                split_b(1)
                inverse_deviation_x1(Tile(1))
                divide(Tile(2), 0)
                divide(Tile(2), 1)
                split_b(2)
                split_b(3)
                inverse_deviation(Tile(3))
                split_xn(Tile(3))
                inverse_deviation_x1(Tile(2))

            def step(i, prep, attend, route, second, third):
                if attend:
                    divide(i, 0)
                    divide(i, 1)
                if prep:
                    inverse_deviation(i + 1)
                    split_xn(i + 1)
                if attend:
                    inverse_deviation_x1(i)

            ramp()
            steps(pool, step)

        @block.scalar
        def _(act):
            act.dma_start(wq[:], Wq).then_inc(qk_in, 16)
            act.dma_start(wk2[:], Wk.unsqueeze(1).to_broadcast([C, 2, C])).then_inc(qk_in, 16)
            for n, g in enumerate((g_xattn, g_ffn)):
                act.dma_start(gates_in[:, n:n + 1], g.rearrange("(a n) -> a n", a=1).to_broadcast([P, 1])).then_inc(g_in, 16)
            act.wait_ge(g_in, 32)
            nc.scalar.activation(tanh_g[:], gates_in[:], ACT.Tanh).then_inc(tanh_made, 1)

            def split_a(groups):
                for g in groups:
                    c, half = a_group(g)
                    col = K + half * 512
                    act.wait_ge(a_t, g + 1)
                    nc.scalar.activation(a_hi[:, c, col:col + 512], a_banks[g][:], ACT.Copy).then_inc(a_hi_made, 1)

            def split_b(c):
                act.wait_ge(b_in[c], 16 * RPC)
                nc.scalar.activation(b_hi[:, :, c * P:(c + 1) * P], b_view[:, c, :, :, 0], ACT.Copy).then_inc(b_hi_made, 1)

            def split_xn(p):
                after(act, xn_made, p.count(1, 1))
                nc.scalar.activation(xn_hi[p.parity][:], xn[:], ACT.Copy).then_inc(xn_hi_made, 1)

            def split_g(p, bank):
                after(act, g_made, p.count(1, 1))
                for b in range(2):
                    g = nc.scalar.activation(g_hi[p.parity][b * C:(b + 1) * C, b, :], bank[b * C:(b + 1) * C, 0:M], ACT.Copy)
                g.then_inc(g_hi_made, 1)

            def split_v(p, bank):
                after(act, v_made, p.count(1, 1))
                nc.scalar.activation(v_hi[p.parity][:].rearrange(v_blocks, c=C)[:, ::3, :],
                                     bank[:, P:2 * P].rearrange(v_blocks, c=C), ACT.Copy).then_inc(v_hi_made, 1)

            def exps(t, s):
                after(act, max_made, t.count(2, s + 1))
                after(act, norm_made, t.count(2, s - 1))
                for q in range(4):
                    e = nc.scalar.activation(prob[:, s, q], ps_e[s][:, q * M:(q + 1) * M], ACT.Exp,
                                             bias=minus_max[:, s, q:q + 1], accum_out=prob_sum[:, s, q:q + 1])
                e.then_inc(exp_made, 1)

            def high_hg(pair, g):
                after(act, hg_made, pair.pair_count(GROUPS, g + 1))
                if g == 0:
                    after(act, out_made, pair.count(1))
                nc.scalar.activation(hgt_hi[:, 2 * g + 2:2 * g + 4, :].rearrange("p j t -> p (j t)"), hg[:, g % 2, :],
                                     ACT.Copy).then_inc(hgt_hi_made, 1)

            def pt_half(t, s):
                after(act, pt_made, t.count(2, s + 1))
                nc.scalar.activation(pt_hi[:, :, s * 256:(s + 1) * 256], ps_pt[:].rearrange("p (b n) -> p b n", b=2), ACT.Copy).then_inc(pt_hi_made, 1)

            def high_xft(f):
                after(act, xf_turned, f.count(1, 1))
                after(act, h_made, f.pair_count(GROUPS))
                nc.scalar.activation(xft_hi[:, :, f.parity * P:(f.parity + 1) * P],
                                     ps_yx[:].rearrange("p (c t) -> p c t", c=NCH), ACT.Copy).then_inc(xft_hi_made, 1)

            def high_first(f):
                after(act, gates_turned, f.count(1, 1))
                after(act, hg_made, f.pair_count(GROUPS))
                nc.scalar.activation(gates_t[:, f.parity * P:(f.parity + 1) * P], ps_s[:, 0:P], ACT.Copy).then_inc(gates_t_made, 1)
                after(act, out_made, f.count(1, -1))
                nc.scalar.activation(hgt_hi[:, 0:2, f.parity * P:(f.parity + 1) * P],
                                     ps_s[:, P:3 * P].rearrange("p (j t) -> p j t", j=2), ACT.Copy).then_inc(first_hi_made, 1)

            def exp_scores(f):
                after(act, top_step, f.count(9, 5))
                nc.scalar.activation(gate_exp[:], scores[:], ACT.Exp, bias=minus_top[:]).then_inc(gate_exp_made, 1)

            def hold_x1(t):
                after(act, x1_made, t.count(1, 1))
                after(act, result_made, (t + -2).count(1, 1))
                nc.scalar.activation(x1_held[t.parity][:], x1[t.parity][:], ACT.Copy).then_inc(held, 1)

            def ramp():
                act.wait_ge(zeroed, 8)
                split_xn(Tile(0))
                split_g(Tile(0), ps_gv)
                split_g(Tile(1), ps_s)
                split_v(Tile(0), ps_out)
                act.wait_ge(wr_t, 1)
                nc.scalar.activation(a_hi[:, :, 0:K], ps_pt[:, 0:DCH * K].rearrange("p (c k) -> p c k", c=DCH), ACT.Copy).then_inc(wr_hi_made, 1)
                split_xn(Tile(1))
                split_v(Tile(1), ps_h0)
                exps(Tile(0), 0)
                exps(Tile(0), 1)
                exps(Tile(1), 0)
                pt_half(Tile(0), 0)
                split_a(range(0, 2))
                pt_half(Tile(0), 1)
                split_a(range(2, 4))
                exps(Tile(1), 1)
                split_a(range(4, 6))
                pt_half(Tile(1), 0)
                split_b(0)
                pt_half(Tile(1), 1)
                high_xft(Tile(0))
                after(act, v_made, 3)
                split_g(Tile(2), ps_gv)
                split_v(Tile(2), ps_gv)
                split_b(1)
                split_b(2)
                split_xn(Tile(2))
                exp_scores(Tile(0))
                split_a(range(6, A_GROUPS))
                high_first(Tile(0))
                exps(Tile(2), 0)
                high_xft(Tile(1))
                exps(Tile(2), 1)
                pt_half(Tile(2), 0)
                split_b(3)
                after(act, v_made, 4)
                split_g(Tile(3), ps_gv)
                split_v(Tile(3), ps_gv)
                hold_x1(Tile(0))
                exp_scores(Tile(1))
                pt_half(Tile(2), 1)
                high_first(Tile(1))
                split_xn(Tile(3))
                high_hg(Tile(0), 0)
                high_hg(Tile(0), 1)

            def step(i, prep, attend, route, second, third):
                pair = i + (-2 - i.parity)
                odd = i.parity == 1
                if attend:
                    exps(i, 0)
                if route:
                    high_xft(i + -1)
                if attend:
                    exps(i, 1)
                    pt_half(i, 0)
                if odd and third:
                    high_hg(pair, 2)
                if prep:
                    after(act, v_made, (i + 1).count(1, 1))
                    split_g(i + 1, ps_gv)
                    split_v(i + 1, ps_gv)
                if second:
                    hold_x1(i + -2)
                if attend:
                    pt_half(i, 1)
                if odd and prep:
                    split_xn(i + 1)
                if route:
                    exp_scores(i + -1)
                if not odd and prep:
                    split_xn(i + 1)
                if route:
                    high_first(i + -1)
                if not odd and second:
                    high_hg(pair, 0)
                    high_hg(pair, 1)

            ramp()
            steps(act, step)

        @block.vector
        def _(dve):
            for u in range(2):
                nc.vector.memset(g_hi[u][:].bitcast(F32), 0.0).then_inc(zeroed, 1)
                nc.vector.memset(g_lo[u][:].bitcast(F32), 0.0).then_inc(zeroed, 1)
                nc.vector.memset(v_hi[u][:].bitcast(F32), 0.0).then_inc(zeroed, 1)
                nc.vector.memset(v_lo[u][:].bitcast(F32), 0.0).then_inc(zeroed, 1)
            nc.vector.memset(qk_bd[:], 0.0).then_inc(zeroed, 1)
            nc.vector.memset(wv_bd[:], 0.0).then_inc(zeroed, 1)
            nc.vector.memset(ws_bd[:], 0.0).then_inc(zeroed, 1)

            def split_a(groups):
                for g in groups:
                    c, half = a_group(g)
                    col = K + half * 512
                    dve.wait_ge(a_hi_made, g + 1)
                    nc.vector.tensor_tensor(a_lo[:, c, col:col + 512], a_banks[g][:],
                                            a_hi[:, c, col:col + 512].bitcast(F32), ALU.subtract).then_inc(a_lo_made, 1)

            def split_g(p, bank):
                for b in range(2):
                    own = slice(b * C, (b + 1) * C)
                    g = nc.vector.tensor_tensor(g_lo[p.parity][own, b, :], bank[own, 0:M], g_hi[p.parity][own, b, :].bitcast(F32), ALU.subtract)
                g.then_inc(g_lo_made, 1)

            def split_v(p, bank):
                nc.vector.tensor_tensor(v_lo[p.parity][:].rearrange(v_blocks, c=C)[:, ::3, :], bank[:, P:2 * P].rearrange(v_blocks, c=C),
                                        v_hi[p.parity][:].bitcast(F32).rearrange(v_blocks, c=C)[:, ::3, :], ALU.subtract).then_inc(v_lo_made, 1)

            def statistics(p):
                after(dve, x_in[p.parity], p.dma_count(1))
                nc.vector.bn_stats(stats1[:], xt[p.parity][:]).then_inc(ln1_step, 1)
                after_apart(dve, ln1_step, p.count(2, 1))
                nc.vector.bn_aggr(mean_var1[:], stats1[:]).then_inc(ln1_step, 1)

            def normalize(p):
                after(dve, rstd1_step, p.count(2, 2))
                after(dve, ln1_step, p.count(2, 2))
                after(dve, xn_lo_made, p.count(1))
                nc.vector.tensor_scalar(xn[:], xt[p.parity][:], mean_var1[:, 0:1], rstd1[:, 0:1], ALU.subtract, ALU.mult).then_inc(xn_made, 1)

            def multiply(pair, g):
                after(dve, h_made, pair.pair_count(GROUPS, g + 1))
                after(dve, hgt_lo_made, pair.pair_count(GROUPS, max(g - 1, 0)))
                if g == 0:
                    dve.wait_ge(gates_t_made, pair.count(1, 2))
                nc.vector.tensor_tensor(hg[:, g % 2, :].rearrange("p (j t) -> p j t", j=2),
                                        ps_h[g][:].rearrange("p (j t) -> p j t", j=2),
                                        gates_t[:].unsqueeze(1).to_broadcast([P, 2, 2 * P]), ALU.mult).then_inc(hg_made, 1)

            def low_hg(pair, g):
                after(dve, hgt_hi_made, pair.pair_count(GROUPS, g + 1))
                if g == 0:
                    after(dve, out_made, pair.count(1))
                nc.vector.tensor_tensor(hgt_lo[:, 2 * g + 2:2 * g + 4, :].rearrange("p j t -> p (j t)"), hg[:, g % 2, :],
                                        hgt_hi[:, 2 * g + 2:2 * g + 4, :].rearrange("p j t -> p (j t)").bitcast(F32),
                                        ALU.subtract).then_inc(hgt_lo_made, 1)

            def largest(t, s):
                after(dve, e_made, t.count(2, s + 1))
                nc.vector.tensor_reduce(minus_max[:, s, :], ps_e[s][:].rearrange("p (q m) -> p q m", q=4),
                                        axis=AX_X, op=ALU.max, negate=True).then_inc(max_made, 1)

            def reciprocals(t, s):
                after(dve, exp_made, t.count(2, s + 1))
                nc.vector.reciprocal(prob_rec[:, s, :], prob_sum[:, s, :]).then_inc(rec_made, 1)

            def pt_half(t, s):
                after(dve, pt_hi_made, t.count(2, s + 1))
                half = slice(s * 256, (s + 1) * 256)
                nc.vector.tensor_tensor(pt_lo[:, :, half], ps_pt[:].rearrange("p (b n) -> p b n", b=2),
                                        pt_hi[:, :, half].bitcast(F32), ALU.subtract).then_inc(pt_lo_made, 1)

            def normalize_x1(f):
                after(dve, rstd2_step, f.count(2, 2))
                after(dve, ln2_step, f.count(2, 2))
                nc.vector.tensor_scalar(xf[:], x1[f.parity][:], mean_var2[:, 0:1], rstd2[:, 0:1], ALU.subtract, ALU.mult).then_inc(xf_made, 1)

            def low_xft(f):
                after(dve, xft_hi_made, f.count(1, 1))
                own = slice(f.parity * P, (f.parity + 1) * P)
                nc.vector.tensor_tensor(xft_lo[:, :, own], ps_yx[:].rearrange("p (c t) -> p c t", c=NCH),
                                        xft_hi[:, :, own].bitcast(F32), ALU.subtract).then_inc(xft_lo_made, 1)

            def multiply_first(f):
                after(dve, top_step, f.count(9, 9))
                nc.vector.tensor_tensor(hg_first[:].rearrange("p (r k) -> p r k", k=K),
                                        ps_s[:, K:K + FIRST_ROWS].rearrange("p (r k) -> p r k", k=K),
                                        gates[:, 0:1, :].to_broadcast([P, FIRST_ROWS // K, K]), ALU.mult).then_inc(hg_first_made, 1)

            def low_first(f):
                after(dve, first_hi_made, f.count(1, 1))
                own = slice(f.parity * P, (f.parity + 1) * P)
                nc.vector.tensor_tensor(hgt_lo[:, 0:2, own], ps_s[:, P:3 * P].rearrange("p (j t) -> p j t", j=2),
                                        hgt_hi[:, 0:2, own].bitcast(F32), ALU.subtract).then_inc(first_lo_made, 1)

            def finish(o, bank):
                after(dve, out_made, o.count(1, 1))
                after(dve, held, o.count(1, 1))
                after(dve, stored, o.count(16))
                nc.vector.tensor_tensor(result[o.parity][:], bank[:], x1_held[o.parity][:], ALU.add).then_inc(result_made, 1)

            def add_x(i):
                after(dve, y_made, i.count(1, 1))
                after(dve, held, (i + -2).count(1, 1))
                nc.vector.tensor_tensor(x1[i.parity][:], ps_yx[:], xt[i.parity][:], ALU.add).then_inc(x1_made, 1)
                after(dve, x1_made, i.count(1, 1))
                nc.vector.bn_stats(stats2[:], x1[i.parity][:]).then_inc(ln2_step, 1)
                after_apart(dve, ln2_step, i.count(2, 1))
                nc.vector.bn_aggr(mean_var2[:], stats2[:]).then_inc(ln2_step, 1)

            def first_top(f):
                after(dve, scores_made, f.count(1, 1))
                nc.vector.tensor_copy(scores[:], ps_s[:, 0:K]).then_inc(top_step, 1)
                after_apart(dve, top_step, f.count(9, 1))
                nc.vector.max(top16[:, 0:TOP], scores[:]).then_inc(top_step, 1)

            def second_top(f):
                after_apart(dve, top_step, f.count(9, 2))
                nc.vector.match_replace(scores_less8[:], top16[:, 0:TOP], scores[:], REPLACED).then_inc(top_step, 1)
                after_apart(dve, top_step, f.count(9, 3))
                nc.vector.max(top16[:, TOP:2 * TOP], scores_less8[:]).then_inc(top_step, 1)
                nc.vector.tensor_scalar(minus_top[:], top16[:, 0:1], -1.0, None, ALU.mult).then_inc(top_step, 1)
                after_apart(dve, top_step, f.count(9, 5))
                nc.vector.match_replace(scores_less16[:], top16[:, TOP:2 * TOP], scores_less8[:], REPLACED).then_inc(top_step, 1)

            def make_gates(f):
                after(dve, top_step, f.count(9, 6))
                after(dve, gate_exp_made, f.count(1, 1))
                nc.vector.scalar_tensor_tensor(gate[:], scores_less16[:], REPLACED, gate_exp[:], ALU.is_le, ALU.mult,
                                               accum_out=gate_sum[:]).then_inc(top_step, 1)
                after(dve, top_step, f.count(9, 7))
                nc.vector.reciprocal(gate_rec[:], gate_sum[:]).then_inc(top_step, 1)
                after(dve, top_step, f.count(9, 8))
                after(dve, gates_turned, f.count(1))
                nc.vector.tensor_scalar(gates[:], gate[:].unsqueeze(1).to_broadcast([P, 2, K]), gate_rec[:], gate_factor[:],
                                        ALU.mult, ALU.mult).then_inc(top_step, 1)

            def ramp():
                statistics(Tile(0))
                dve.wait_ge(zeroed, 11)
                dve.wait_ge(qk_t, 1)
                for b in range(2):
                    own = slice(b * C, (b + 1) * C)
                    nc.vector.tensor_scalar(qk_bd[own, own], ps_e[0][own, 0:C], float(C) ** -0.5, None, ALU.mult).then_inc(qk_ready, 1)
                normalize(Tile(0))
                dve.wait_ge(g_hi_made, 1)
                split_g(Tile(0), ps_gv)
                dve.wait_ge(xn_hi_made, 1)
                nc.vector.tensor_tensor(xn_lo[0][:], xn[:], xn_hi[0][:].bitcast(F32), ALU.subtract).then_inc(xn_lo_made, 1)
                dve.wait_ge(tanh_made, 1)
                nc.vector.tensor_scalar(gate_factor[:], tanh_g[:, 1:2], FFN_SCALING, None, ALU.mult).then_inc(factor_made, 1)
                dve.wait_ge(vs_t, 1)
                for b in range(2):
                    own = slice(b * C, (b + 1) * C)
                    nc.vector.tensor_scalar(wv_bd[own, own], ps_e[1][own, 0:C], tanh_g[own, 0:1], None, ALU.mult).then_inc(wv_ready, 1)
                for b in range(2):
                    own = slice(b * C, (b + 1) * C)
                    nc.vector.tensor_scalar(ws_bd[own, own], ps_e[1][own, C:2 * C], tanh_g[own, 0:1], None, ALU.mult).then_inc(ws_ready, 1)
                statistics(Tile(1))
                dve.wait_ge(g_hi_made, 2)
                split_g(Tile(1), ps_s)
                normalize(Tile(1))
                dve.wait_ge(ws_ready, 2)
                nc.vector.tensor_copy(ws_hi[:], ws_bd[:]).then_inc(ws_ready, 1)
                dve.wait_ge(ws_ready, 3)
                nc.vector.tensor_tensor(ws_lo[:], ws_bd[:], ws_hi[:].bitcast(F32), ALU.subtract).then_inc(ws_ready, 1)
                largest(Tile(0), 0)
                largest(Tile(0), 1)
                dve.wait_ge(v_hi_made, 1)
                split_v(Tile(0), ps_out)
                dve.wait_ge(wr_hi_made, 1)
                nc.vector.tensor_tensor(a_lo[:, :, 0:K], ps_pt[:, 0:DCH * K].rearrange("p (c k) -> p c k", c=DCH),
                                        a_hi[:, :, 0:K].bitcast(F32), ALU.subtract).then_inc(wr_lo_made, 1)
                dve.wait_ge(v_hi_made, 2)
                split_v(Tile(1), ps_h0)
                reciprocals(Tile(0), 0)
                largest(Tile(1), 0)
                reciprocals(Tile(0), 1)
                largest(Tile(1), 1)
                reciprocals(Tile(1), 0)
                pt_half(Tile(0), 0)
                split_a(range(0, 2))
                pt_half(Tile(0), 1)
                split_a(range(2, 4))
                reciprocals(Tile(1), 1)
                add_x(Tile(0))
                pt_half(Tile(1), 0)
                normalize_x1(Tile(0))
                split_a(range(4, 5))
                pt_half(Tile(1), 1)
                low_xft(Tile(0))
                statistics(Tile(2))
                dve.wait_ge(v_hi_made, 3)
                split_g(Tile(2), ps_gv)
                split_v(Tile(2), ps_gv)
                split_a(range(5, 6))
                normalize(Tile(2))
                first_top(Tile(0))
                second_top(Tile(0))
                dve.wait_ge(factor_made, 1)
                make_gates(Tile(0))
                multiply_first(Tile(0))
                add_x(Tile(1))
                largest(Tile(2), 0)
                low_first(Tile(0))
                normalize_x1(Tile(1))
                largest(Tile(2), 1)
                reciprocals(Tile(2), 0)
                split_a(range(6, 7))
                low_xft(Tile(1))
                reciprocals(Tile(2), 1)
                split_a(range(7, A_GROUPS))
                pt_half(Tile(2), 0)
                first_top(Tile(1))
                second_top(Tile(1))
                make_gates(Tile(1))
                multiply_first(Tile(1))
                dve.wait_ge(v_hi_made, 4)
                split_g(Tile(3), ps_gv)
                split_v(Tile(3), ps_gv)
                statistics(Tile(3))
                pt_half(Tile(2), 1)
                multiply(Tile(0), 0)
                normalize(Tile(3))
                low_first(Tile(1))
                multiply(Tile(0), 1)
                add_x(Tile(2))
                low_hg(Tile(0), 0)

            def step(i, prep, attend, route, second, third):
                p, f, o = i + 1, i + -1, i + -3
                pair = i + (-2 - i.parity)
                odd = i.parity == 1
                if route:
                    normalize_x1(f)
                if attend:
                    largest(i, 0)
                if odd and third:
                    low_hg(pair, 1)
                    multiply(pair, 2)
                if attend:
                    largest(i, 1)
                    reciprocals(i, 0)
                if route:
                    low_xft(f)
                if attend:
                    reciprocals(i, 1)
                if not odd and third:
                    finish(o, ps_h0)
                if attend:
                    pt_half(i, 0)
                if odd and third:
                    low_hg(pair, 2)
                if prep:
                    after(dve, v_hi_made, p.count(1, 1))
                    split_g(p, ps_gv)
                    split_v(p, ps_gv)
                if odd and prep:
                    statistics(p)
                if route:
                    first_top(f)
                if attend:
                    pt_half(i, 1)
                if odd and prep:
                    normalize(p)
                if route:
                    second_top(f)
                if odd and third:
                    finish(o, ps_out)
                if not odd and prep:
                    statistics(p)
                if route:
                    make_gates(f)
                    multiply_first(f)
                if not odd and prep:
                    normalize(p)
                if not odd and second:
                    multiply(pair, 0)
                if route and not odd:
                    low_first(f)
                if not odd and second:
                    multiply(pair, 1)
                if attend:
                    add_x(i)
                if route and odd:
                    low_first(f)
                if not odd and second:
                    low_hg(pair, 0)

            ramp()
            steps(dve, step)

        @block.tensor
        def _(pe):
            def a_transposes(groups):
                pe.wait_ge(a_in, 16 * RPC)
                for g in groups:
                    if g >= 3:
                        pe.wait_ge(a_lo_made, max(n for n in range(g) if a_banks[n] is a_banks[g]) + 1)
                    c, half = a_group(g)
                    for j in range(4):
                        w = nc.tensor.transpose(a_banks[g][:, j * P:(j + 1) * P],
                                                a_raw[:, 4 * half + j, c * P:(c + 1) * P], ident[:])
                    w.then_inc(a_t, 1)

            def g_product(p, bank):
                after(pe, ctx_in[p.parity], p.dma_count(1))
                nc.tensor.matmul(bank[:, 0:M], qk_bd[:], ct[p.parity][:], start=True, stop=True).then_inc(g_made, 1)

            def v_product(p, bank):
                nc.tensor.matmul(bank[:, P:2 * P], ct[p.parity][:], wv_bd[:], start=True, stop=True).then_inc(v_made, 1)

            def split_product(dst, hi_l, lo_l, hi_r, lo_r, start, stop):
                nc.tensor.matmul(dst, hi_l, hi_r, start=start, stop=False)
                nc.tensor.matmul(dst, hi_l, lo_r, start=False, stop=False)
                return nc.tensor.matmul(dst, lo_l, hi_r, start=False, stop=stop)

            def energies(t, s):
                v = t.parity
                after(pe, xn_lo_made, t.count(1, 1))
                after(pe, g_lo_made, t.count(1, 1))
                after(pe, exp_made, t.count(2, s - 1))
                for q in range(2):
                    n = (2 * s + q) * P
                    w = split_product(ps_e[s][:, q * 2 * M:(q + 1) * 2 * M],
                                      xn_hi[v][:, n:n + P], xn_lo[v][:, n:n + P],
                                      g_hi[v][:].rearrange("p b m -> p (b m)"), g_lo[v][:].rearrange("p b m -> p (b m)"),
                                      True, True)
                w.then_inc(e_made, 1)

            def prob_transposes(t, s):
                after(pe, norm_made, t.count(2, s + 1))
                after(pe, pt_lo_made, t.count(2, s))
                for q in range(2):
                    for b in range(2):
                        w = nc.tensor.transpose(ps_pt[:, b * 256 + q * P:b * 256 + (q + 1) * P], prob_n[:, s, 2 * q + b, :], ident[:])
                w.then_inc(pt_made, 1)

            def xf_transposes(f):
                after(pe, xf_made, f.count(1, 1))
                for c in range(NCH):
                    w = nc.tensor.transpose(ps_yx[:, c * P:(c + 1) * P], xf[:, c * P:(c + 1) * P], ident[:])
                w.then_inc(xf_turned, 1)

            def score_product(f):
                turned = slice(f.parity * P, (f.parity + 1) * P)
                after(pe, xft_hi_made, f.count(1, 1))
                after(pe, first_lo_made, f.count(1))
                for c in range(DCH):
                    nc.tensor.matmul(ps_s[:, 0:K + FIRST_ROWS], xft_hi[:, c, turned], a_hi[:, c, 0:K + FIRST_ROWS], start=c == 0, stop=False)
                    nc.tensor.matmul(ps_s[:, 0:K + FIRST_ROWS], xft_hi[:, c, turned], a_lo[:, c, 0:K + FIRST_ROWS], start=False, stop=False)
                after(pe, xft_lo_made, f.count(1, 1))
                for c in range(DCH):
                    w = nc.tensor.matmul(ps_s[:, 0:K + FIRST_ROWS], xft_lo[:, c, turned], a_hi[:, c, 0:K + FIRST_ROWS], start=False, stop=c == DCH - 1)
                w.then_inc(scores_made, 1)

            def gate_transposes(f):
                after(pe, hg_first_made, f.count(1, 1))
                nc.tensor.transpose(ps_s[:, 0:P], gates[:].rearrange("p r k -> p (r k)"), ident[:])
                for j in range(FIRST_ROWS // P):
                    w = nc.tensor.transpose(ps_s[:, (j + 1) * P:(j + 2) * P], hg_first[:, j * P:(j + 1) * P], ident[:])
                w.then_inc(gates_turned, 1)

            def hidden(pair, g, between=None):
                if g == 0:
                    after(pe, result_made, pair.count(1))
                if g == 2:
                    after(pe, hg_made, pair.pair_count(GROUPS, 1))
                for n in range(2):
                    if between and n == 1:
                        between()
                    first = K + FIRST_ROWS + (2 * g + n) * P
                    for c in range(DCH):
                        w = split_product(ps_h[g][:, n * 2 * P:(n + 1) * 2 * P], a_hi[:, c, first:first + P], a_lo[:, c, first:first + P],
                                          xft_hi[:, c], xft_lo[:, c], c == 0, c == DCH - 1)
                w.then_inc(h_made, 1)

            def out_quarter(pair, n, between=None):
                t, half = n // 2, n % 2
                bank = (ps_out, ps_h0)[t]
                if n == 0:
                    after(pe, first_lo_made, pair.count(1, 2))
                    after(pe, hgt_lo_made, pair.pair_count(GROUPS, 1))
                    after(pe, hg_made, pair.pair_count(GROUPS, 2))
                if n == 2:
                    after(pe, hg_made, pair.pair_count(GROUPS, 3))
                own = slice(t * P, (t + 1) * P)
                for j in range(4 * half, 4 * half + 4):
                    if n == 1 and j % 2 == 0:
                        after(pe, hgt_lo_made, pair.pair_count(GROUPS, j // 2))
                    if between and j == 4 * half + 2:
                        between()
                    w = split_product(bank[:], hgt_hi[:, j, own], hgt_lo[:, j, own], b_hi[:, j], b_lo[:, j], j == 0, j == KCH - 1)
                if half == 1:
                    w.then_inc(out_made, 1)

            def attention(i):
                u = i.parity
                after(pe, xft_lo_made, i.count(1))
                split_product(ps_yx[:], ws_hi[:], ws_lo[:], xn_hi[u][:], xn_lo[u][:], True, False)
                after(pe, v_lo_made, i.count(1, 1))
                after(pe, pt_lo_made, i.count(2, 2))
                for b in range(2):
                    half = slice(b * P, (b + 1) * P)
                    w = split_product(ps_yx[:], v_hi[u][:, half], v_lo[u][:, half], pt_hi[:, b], pt_lo[:, b], False, b == 1)
                w.then_inc(y_made, 1)

            def products_of_ctx(p):
                after(pe, v_lo_made, p.count(1))
                g_product(p, ps_gv)
                v_product(p, ps_gv)

            def ramp():
                pe.wait_ge(const_made, 3)
                flat = "o b c -> o (b c)"
                pe.wait_ge(qk_in, 32)
                nc.tensor.matmul(ps_e[0][:, 0:C], wk2[:].rearrange(flat), wq[:], start=True, stop=True).then_inc(qk_t, 1)
                pe.wait_ge(vs_in, 32)
                nc.tensor.transpose(ps_e[1][:, 0:C], wv2[:].rearrange(flat), ident[0:C, 0:C])
                nc.tensor.transpose(ps_e[1][:, C:2 * C], ws2[:].rearrange(flat), ident[0:C, 0:C]).then_inc(vs_t, 1)
                pe.wait_ge(qk_ready, 2)
                g_product(Tile(0), ps_gv)
                g_product(Tile(1), ps_s)
                pe.wait_ge(wv_ready, 2)
                v_product(Tile(0), ps_out)
                pe.wait_ge(wr_in, 16)
                for c in range(DCH):
                    w = nc.tensor.transpose(ps_pt[:, c * K:(c + 1) * K], wr[:, c * P:(c + 1) * P], ident[0:K, 0:K])
                w.then_inc(wr_t, 1)
                v_product(Tile(1), ps_h0)
                pe.wait_ge(zeroed, 11)
                pe.wait_ge(ws_ready, 2)
                energies(Tile(0), 0)
                energies(Tile(0), 1)
                energies(Tile(1), 0)
                pe.wait_ge(wr_lo_made, 1)
                prob_transposes(Tile(0), 0)
                energies(Tile(1), 1)
                pe.wait_ge(v_lo_made, 2)
                a_transposes(range(0, 2))
                prob_transposes(Tile(0), 1)
                a_transposes(range(2, 5))
                pe.wait_ge(ws_ready, 4)
                attention(Tile(0))
                a_transposes(range(5, 6))
                prob_transposes(Tile(1), 0)
                prob_transposes(Tile(1), 1)
                xf_transposes(Tile(0))
                products_of_ctx(Tile(2))
                pe.wait_ge(a_lo_made, DCH)
                score_product(Tile(0))
                a_transposes(range(6, A_GROUPS))
                attention(Tile(1))
                energies(Tile(2), 0)
                gate_transposes(Tile(0))
                energies(Tile(2), 1)
                xf_transposes(Tile(1))
                products_of_ctx(Tile(3))
                score_product(Tile(1))
                prob_transposes(Tile(2), 0)
                pe.wait_ge(a_lo_made, A_GROUPS)
                hidden(Tile(0), 0)
                prob_transposes(Tile(2), 1)
                hidden(Tile(0), 1)
                gate_transposes(Tile(1))
                attention(Tile(2))
                hidden(Tile(0), 2)
                pe.wait_ge(b_lo_made, DCH)

            def step(i, prep, attend, route, second, third):
                p, f = i + 1, i + -1
                pair = i + (-2 - i.parity)
                odd = i.parity == 1
                if attend:
                    energies(i, 0)
                    energies(i, 1)
                    xf_transposes(f)
                if prep:
                    products_of_ctx(p)
                if odd and third:
                    out_quarter(pair, 0)
                elif second:
                    out_quarter(pair + -2, 3, between=None if attend else lambda: xf_transposes(f))
                if attend:
                    prob_transposes(i, 0)
                if route:
                    score_product(f)
                if attend:
                    prob_transposes(i, 1)
                if not odd and second:
                    hidden(pair, 0)
                    hidden(pair, 1, between=None if attend else lambda: gate_transposes(f))
                if odd and third:
                    out_quarter(pair, 1)
                if attend and not odd:
                    gate_transposes(f)
                if attend:
                    attention(i)
                if not odd and second:
                    hidden(pair, 2)
                if odd and third:
                    if attend:
                        out_quarter(pair, 2, between=lambda: gate_transposes(f))
                    else:
                        out_quarter(pair, 2)
                        out_quarter(pair, 3)

            ramp()
            steps(pe, step)


INPUTS = ["x", "ctx_1024", "g_xattn", "g_ffn", "L0_xattn_Wq", "L0_xattn_Wk", "L0_xattn_Wv", "L0_xattn_Wskip",
          "L0_ffn_A", "L0_ffn_B", "L0_ffn_Wr"]


def kernel(**inputs):
    import numpy as np
    import concourse.bacc as bacc
    from concourse.bass_utils import run_bass_kernel_spmd

    nc = bacc.Bacc("TRN2", target_bir_lowering=False, num_devices=1)
    arrays, args = {}, []
    for name in INPUTS:
        a = np.ascontiguousarray(inputs[name])
        arrays[f"in_{name}"] = a
        args.append(nc.dram_tensor(f"in_{name}", a.shape, mybir.dt.from_np(a.dtype), kind="ExternalInput").ap())
    out = nc.dram_tensor("out_x", arrays["in_x"].shape, F32, kind="ExternalOutput").ap()
    flamingo_block(nc, *args, out)
    r = run_bass_kernel_spmd(nc, [arrays], core_ids=[0])
    return r.results[0]["out_x"]
```
